# Optimizing a Trainium2 kernel written in Bass

```python
import numpy as np
import jax
import jax.numpy as jnp

def _softmax(x, axis=-1):
    return jax.nn.softmax(x, axis=axis)

def _gelu(x):
    return jax.nn.gelu(x, approximate=True)

def _silu(x):
    return jax.nn.silu(x)

def _sigmoid(x):
    return jax.nn.sigmoid(x)

def _layernorm(x, axis=-1, eps=1e-05):
    m = jnp.mean(x, axis=axis, keepdims=True)
    v = jnp.var(x, axis=axis, keepdims=True)
    return (x - m) / jnp.sqrt(v + eps)

def _scatter_add(tgt, idx, src, axis=0):
    return tgt.at[idx].add(src)

def _segment_sum(src, seg, n):
    return jax.ops.segment_sum(src, seg, n)
kernel_name = 'mk_flamingo_gated_d1_seqx_r4_e34afb'

def setup_inputs(seed: int=0):
    np.random.seed(seed)
    _w = jnp.asarray

    def _rec_inputs():
        import jax
        import jax.numpy as jnp
        _rk = jax.random.key(seed)
        x = -0.0002928 + 1 * jax.random.normal(jax.random.fold_in(_rk, 1), (2, 1024, 256), jnp.float32)
        _lenS = 1024 - jax.random.randint(jax.random.fold_in(_rk, 7), (2,), 0, max(1, 1024 // 4) + 1, jnp.int32)
        _lenS2 = 77 - jax.random.randint(jax.random.fold_in(_rk, 8), (2,), 0, max(1, 77 // 4) + 1, jnp.int32)
        _ctx_1024P = jax.random.normal(jax.random.fold_in(_rk, 11), (2, 16, 256), jnp.float32)
        _ctx_1024c = jax.random.dirichlet(jax.random.fold_in(_rk, 511), 0.3 * jnp.ones((16,), jnp.float32), (2, 77))
        _ctx_1024t = jnp.einsum('bsk,bkd->bsd', _ctx_1024c, _ctx_1024P)
        _ctx_1024t = _ctx_1024t * jax.lax.rsqrt(jnp.mean(jnp.square(_ctx_1024t)) + 1e-12) * 0.953939
        ctx_1024 = -1.39393e-06 + 0.999914 * (_ctx_1024t + 0.3 * jax.random.normal(jax.random.fold_in(_rk, 611), (2, 77, 256), jnp.float32))
        _g = jax.random.normal(jax.random.fold_in(_rk, 9001), (2, 1), jnp.float32)
        _g = jnp.sign(_g) * jnp.maximum(jnp.abs(_g), 1.0) + (_g == 0) * 1.0
        g_xattn = _g[0]
        g_ffn = _g[1]
        return (x, ctx_1024, g_xattn, g_ffn)
    x, ctx_1024, g_xattn, g_ffn = _rec_inputs()

    def _L0_xattn_setup():
        import jax, jax.numpy as jnp
        import numpy as np
        D_MODEL = 256
        N_HEADS = 16
        HEAD_DIM = D_MODEL // N_HEADS

        def sparsemax(x):
            x = x - jnp.max(x, axis=-1, keepdims=True)
            zs = -jnp.sort(-x, axis=-1)
            L = x.shape[-1]
            rho = jnp.arange(1, L + 1, dtype=x.dtype)
            cssv = jnp.cumsum(zs, axis=-1) - 1.0
            support = zs > cssv / rho
            k = jnp.maximum(jnp.sum(support, axis=-1, keepdims=True), 1)
            tau = jnp.take_along_axis(cssv, k - 1, axis=-1) / k.astype(x.dtype)
            return jnp.clip(x - tau, 0.0)

        def _split_heads(x):
            B, L, _ = x.shape
            return x.reshape(B, L, N_HEADS, HEAD_DIM).transpose(0, 2, 1, 3)
        key = jax.random.key(seed)
        ks = jax.random.split(key, 11)
        B, L = (2, 512)
        s = 0.02
        inp = {'q': jax.random.normal(ks[0], (B, L, D_MODEL), jnp.float32), 'k': jax.random.normal(ks[1], (B, L, D_MODEL), jnp.float32), 'v': jax.random.normal(ks[2], (B, L, D_MODEL), jnp.float32), 'Wq': jax.random.normal(ks[3], (D_MODEL, D_MODEL), jnp.float32) * s, 'bq': jnp.zeros((D_MODEL,), jnp.float32), 'Wk': jax.random.normal(ks[4], (D_MODEL, D_MODEL), jnp.float32) * s, 'bk': jnp.zeros((D_MODEL,), jnp.float32), 'Wv': jax.random.normal(ks[5], (D_MODEL, D_MODEL), jnp.float32) * s, 'bv': jnp.zeros((D_MODEL,), jnp.float32), 'Wo': jax.random.normal(ks[6], (D_MODEL, D_MODEL), jnp.float32) * s, 'bo': jnp.zeros((D_MODEL,), jnp.float32)}
        return inp
    _L0_xattn_all = _L0_xattn_setup()
    _L0_xattn_in = {k: v for k, v in _L0_xattn_all.items() if k in ('Wq', 'bq', 'Wk', 'bk', 'Wv', 'bv', 'Wo', 'bo')}
    del _L0_xattn_all

    def _L0_ffn_setup():
        import math
        import jax, jax.numpy as jnp
        import numpy as np
        NUM_EXPERTS = 8
        CAPACITY_FACTOR = 1.5
        key = jax.random.key(seed)
        ks = jax.random.split(key, 4)
        B, T, D, F, E = (4, 512, 256, 1024, NUM_EXPERTS)
        scale = 0.02
        return {'x': jax.random.normal(ks[0], (B, T, D), dtype=jnp.float32), 'router_w': jax.random.normal(ks[1], (E, D), dtype=jnp.float32) * scale, 'w1': jax.random.normal(ks[2], (E, D, F), dtype=jnp.float32) * scale, 'b1': jnp.zeros((E, F), dtype=jnp.float32), 'w2': jax.random.normal(ks[3], (E, F, D), dtype=jnp.float32) * scale, 'b2': jnp.zeros((E, D), dtype=jnp.float32)}
    _L0_ffn_all = _L0_ffn_setup()
    _L0_ffn_in = {k: v for k, v in _L0_ffn_all.items() if k in ('router_w', 'w1', 'b1', 'w2', 'b2')}
    del _L0_ffn_all
    return {'x': x, 'ctx_1024': ctx_1024, 'g_xattn': g_xattn, 'g_ffn': g_ffn, 'L0_xattn_Wq': _L0_xattn_in['Wq'], 'L0_xattn_bq': _L0_xattn_in['bq'], 'L0_xattn_Wk': _L0_xattn_in['Wk'], 'L0_xattn_bk': _L0_xattn_in['bk'], 'L0_xattn_Wv': _L0_xattn_in['Wv'], 'L0_xattn_bv': _L0_xattn_in['bv'], 'L0_xattn_Wo': _L0_xattn_in['Wo'], 'L0_xattn_bo': _L0_xattn_in['bo'], 'L0_ffn_router_w': _L0_ffn_in['router_w'], 'L0_ffn_w1': _L0_ffn_in['w1'], 'L0_ffn_b1': _L0_ffn_in['b1'], 'L0_ffn_w2': _L0_ffn_in['w2'], 'L0_ffn_b2': _L0_ffn_in['b2']}

def reference(x, ctx_1024, g_xattn, g_ffn, L0_xattn_Wq, L0_xattn_bq, L0_xattn_Wk, L0_xattn_bk, L0_xattn_Wv, L0_xattn_bv, L0_xattn_Wo, L0_xattn_bo, L0_ffn_router_w, L0_ffn_w1, L0_ffn_b1, L0_ffn_w2, L0_ffn_b2):
    import jax
    import jax.numpy as jnp

    def _L0_xattn_ref(q, k, v, Wq, bq, Wk, bk, Wv, bv, Wo, bo):
        import jax, jax.numpy as jnp
        import numpy as np
        D_MODEL = 256
        N_HEADS = 16
        HEAD_DIM = D_MODEL // N_HEADS

        def sparsemax(x):
            x = x - jnp.max(x, axis=-1, keepdims=True)
            zs = -jnp.sort(-x, axis=-1)
            L = x.shape[-1]
            rho = jnp.arange(1, L + 1, dtype=x.dtype)
            cssv = jnp.cumsum(zs, axis=-1) - 1.0
            support = zs > cssv / rho
            k = jnp.maximum(jnp.sum(support, axis=-1, keepdims=True), 1)
            tau = jnp.take_along_axis(cssv, k - 1, axis=-1) / k.astype(x.dtype)
            return jnp.clip(x - tau, 0.0)

        def _split_heads(x):
            B, L, _ = x.shape
            return x.reshape(B, L, N_HEADS, HEAD_DIM).transpose(0, 2, 1, 3)
        qh = _split_heads(q @ Wq + bq)
        kh = _split_heads(k @ Wk + bk)
        vh = _split_heads(v @ Wv + bv)
        scale = HEAD_DIM ** (-0.5)
        scores = jnp.einsum('bhqd,bhkd->bhqk', qh, kh) * scale
        attn = sparsemax(scores)
        out = jnp.einsum('bhqk,bhkd->bhqd', attn, vh)
        B, L = (q.shape[0], q.shape[1])
        out = out.transpose(0, 2, 1, 3).reshape(B, L, D_MODEL)
        return out @ Wo + bo

    def _L0_ffn_ref(x, router_w, w1, b1, w2, b2):
        import math
        import jax, jax.numpy as jnp
        import numpy as np
        NUM_EXPERTS = 8
        CAPACITY_FACTOR = 1.5
        B, T, D = x.shape
        E = router_w.shape[0]
        N = B * T
        C = max(math.ceil(CAPACITY_FACTOR * N / E), 1)
        x_flat = x.reshape(N, D)
        logits = x_flat @ router_w.T
        probs = jax.nn.softmax(logits, axis=-1)
        chosen_e = jnp.argmax(probs, axis=-1)
        chosen_p = jnp.max(probs, axis=-1)
        onehot = jax.nn.one_hot(chosen_e, E, dtype=jnp.float32)
        pos = jnp.take_along_axis(jnp.cumsum(onehot, axis=0), chosen_e[:, None], axis=1)[:, 0] - 1.0
        pos = pos.astype(jnp.int32)
        kept = pos < C
        pos_c = jnp.clip(pos, 0, C - 1)
        buf = jnp.zeros((E, C, D), dtype=x.dtype).at[chosen_e, pos_c].add(x_flat * kept[:, None].astype(x.dtype))
        h = jax.nn.gelu(jnp.einsum('ecd,edf->ecf', buf, w1) + b1[:, None, :], approximate=False)
        eo = jnp.einsum('ecf,efd->ecd', h, w2) + b2[:, None, :]
        y = eo[chosen_e, pos_c] * (chosen_p * kept.astype(x.dtype))[:, None]
        return y.reshape(B, T, D)
    x = x + jnp.tanh(g_xattn[0]) * _L0_xattn_ref(_layernorm(x, axis=-1), ctx_1024, ctx_1024, L0_xattn_Wq, L0_xattn_bq, L0_xattn_Wk, L0_xattn_bk, L0_xattn_Wv, L0_xattn_bv, L0_xattn_Wo, L0_xattn_bo)
    x = x + jnp.tanh(g_ffn[0]) * _L0_ffn_ref(_layernorm(x, axis=-1), L0_ffn_router_w, L0_ffn_w1, L0_ffn_b1, L0_ffn_w2, L0_ffn_b2)
    return x

_drawn_inputs = setup_inputs


def setup_inputs(seed=0):
    import zlib

    import numpy as np

    out = dict(_drawn_inputs(seed))
    spreads = {'L0_xattn_bq': (0.0, 0.595),
     'L0_xattn_bk': (0.0, 0.8),
     'L0_xattn_bv': (0.0, 0.311),
     'L0_xattn_bo': (0.0, 0.1),
     'L0_ffn_b1': (0.0, 0.8),
     'L0_ffn_b2': (0.0, 0.413)}
    factors = {'L0_ffn_w1': 2.711}
    for name, (base, spread) in spreads.items():
        noise = np.random.default_rng([zlib.crc32(name.encode()), seed]).standard_normal(out[name].shape)
        drawn = base * np.exp(spread * noise) if base else spread * noise
        out[name] = jnp.asarray(drawn.astype(out[name].dtype))
    for name, factor in factors.items():
        out[name] = (out[name] * factor).astype(out[name].dtype)
    return out
```

```python
from contextlib import ExitStack

import numpy as np

import concourse.bass as bass
from concourse import mybir

ALU = mybir.AluOpType
ACT = mybir.ActivationFunctionType
F32 = mybir.dt.float32
BF16 = mybir.dt.bfloat16
FP16 = mybir.dt.float16
I32 = mybir.dt.int32
U32 = mybir.dt.uint32
AX_X = mybir.AxisListType.X

P = 128
B = 2
T = 1024
N = B * T
D = 256
DH = D // P
H = 16
HD = D // H
HH = H // DH
L = 77
E = 8
F = 1024
FT = F // P
CAP = -(-3 * N // (2 * E))
CT = CAP // P
NCH = N // P
CB = T // P
KT = -(-HH * L // P)
KW = KT * P
W = DH * KW
NT = DH * KT
EPS = 1e-5
PIECES = ((0, 4), (4, NT))

COARSE = 4
FINE = 2
GENERAL = 32
LIMIT = 1e-10
GUESS = (0.0497, -0.1, 0.22)

C_ID = 0
C_TRI = C_ID + P
C_ONE = C_TRI + P
C_HEAD = C_ONE + P
C_V = C_HEAD + HH
C_IND = C_V + KW
C_NEG = C_IND + NT * H
C_IOTA = C_NEG + W
C_REV = C_IOTA + E
C_BASE = C_REV + E
C_ROW = C_BASE + E
C_ALL = C_ROW + 1


def constants():
    c = np.zeros((P, C_ALL), np.float32)
    r = np.arange(P)
    c[:, C_ID:C_ID + P] = np.eye(P)
    c[:, C_TRI:C_TRI + P] = r[:, None] < r[None, :]
    c[:, C_ONE:C_ONE + P] = 1
    c[:, C_HEAD:C_HEAD + HH] = r[:, None] // HD == np.arange(HH)
    hk = np.arange(KW)
    head = np.where(hk < HH * L, hk // L, -1)
    v = (head.reshape(KT, P).T[:, :, None] == (r // HD)[None, None, :])
    c[:, C_V:C_V + KW] = v.reshape(P, KW)
    for g in range(DH):
        hg = np.where(head >= 0, head + g * HH, -1)
        ind = hg.reshape(KT, P).T[:, :, None] == np.arange(H)
        c[:, C_IND + g * KT * H:C_IND + (g + 1) * KT * H] = ind.reshape(P, KT * H)
        for part in range(2):
            c[part * H:(part + 1) * H, C_NEG + g * KW:C_NEG + (g + 1) * KW] = -(hg[None, :] == np.arange(H)[:, None]).astype(np.float32)
    c[:, C_IOTA:C_IOTA + E] = np.arange(E)
    c[:, C_REV:C_REV + E] = E - np.arange(E)
    c[:, C_BASE:C_BASE + E] = np.arange(E) * CAP
    c[:, C_ROW] = E * CAP + r
    return c


class Link:

    def __init__(self, eng, sem):
        self.eng, self.sem, self.n, self.base = eng, sem, 0, 0

    def at(self, base):
        self.base, self.n = base, 0

    def __call__(self, ins):
        self.n += 1
        ins.then_inc(self.sem, 1)
        self.eng.wait_ge(self.sem, self.base + self.n)


def flamingo_layer(nc, x_d, ctx_d, gx_d, gf_d, wq_d, bq_d, wk_d, bk_d, wv_d, bv_d, wo_d, bo_d,
                   rw_d, w1_d, b1_d, w2_d, b2_d, cst_d, out_d):
    with ExitStack() as ctx:
        def sb(name, shape, dt=F32):
            return ctx.enter_context(nc.sbuf_tensor(name, shape, dt))

        def psum(name, shape, dt=F32):
            return ctx.enter_context(nc.psum_tensor(name, shape, dt))

        def sem(name):
            return ctx.enter_context(nc.semaphore(name))

        def sems(name, n=B):
            return [sem(f"{name}{i}") for i in range(n)]

        cst = sb("cst", [P, C_ALL])
        ident = cst[:, C_ID:C_ID + P]
        identb = sb("identb", [P, P], BF16)
        trib = sb("trib", [P, P], BF16)
        onesb = sb("onesb", [P, P], BF16)
        ones_row = cst[0:1, C_ONE:C_ONE + P]
        ind32 = cst[:, C_IND:C_IND + NT * H].rearrange("p (t h) -> p t h", t=NT)
        indb = sb("indb", [P, NT, H], BF16)
        indh = sb("indh", [P, NT, H], FP16)
        negb = sb("negb", [2 * H, W], BF16)
        wq = sb("wq", [P, DH, D])
        wk = sb("wk", [P, DH, D])
        wv = sb("wv", [P, DH, D])
        wo = sb("wo", [P, DH, D])
        rows = sb("rows", [8, P])
        bcol = sb("bcol", [P, 4])
        bqs = sb("bqs", [P, DH])
        bvr = sb("bvr", [1, D])
        bob = sb("bob", [P, D])
        gcol = sb("gcol", [P, 2])
        tg = sb("tg", [P, 2])
        eps = sb("eps", [P, 1])
        rw = sb("rw", [E, D])
        rwT = sb("rwT", [P, DH, E])
        b1r = sb("b1r", [E * FT, P])
        b1T = sb("b1T", [P, E * FT])
        cx = sb("cx", [L, B, D])
        cxT = sb("cxT", [P, B, DH, L])
        cxR = sb("cxR", [P, B, DH, KW])
        kT = sb("kT", [P, B, DH, L])
        ksum = sb("ksum", [P, B * DH])
        KB = sb("KB", [P, B, W])
        VB = sb("VB", [P, B, NT, P])
        x = sb("x", [P, NCH, D])
        x1 = sb("x1", [P, NCH, D])
        stats = sb("stats", [P, NCH, 6])
        mv = sb("mv", [P, NCH, 2])
        sd = sb("sd", [P, NCH])
        rs = sb("rs", [P, NCH])
        xn = sb("xn", [P, B, D])
        xnT = sb("xnT", [P, B, DH, P])
        qT = sb("qT", [P, DH, N])
        r16 = sb("r16", [P, B, W], BF16)
        msk = sb("msk", [P, B, W], BF16)
        rlo = sb("rlo", [P, B, W], FP16)
        r32 = sb("r32", [P, B, W])
        flag = sb("flag", [P, 2])
        flagi = sb("flagi", [1, 1], I32)
        off = sb("off", [P, B, H])
        cnt = sb("cnt", [P, B, H])
        step = sb("step", [P, B, H])
        rest = sb("rest", [P, B, H])
        parts = sb("parts", [P, B, 2 * H], BF16)
        partsT = sb("partsT", [2 * H, B, P], BF16)
        oT = sb("oT", [P, B, DH, P])
        lg = sb("lg", [P, NCH, E])
        lmax = sb("lmax", [P, NCH])
        oh = sb("oh", [P, NCH, E])
        ohb = sb("ohb", [P, NCH, E], BF16)
        t3 = sb("t3", [P, NCH, E])
        t2 = sb("t2", [P, NCH])
        pos = sb("pos", [P, NCH])
        base = sb("base", [P, NCH])
        kept = sb("kept", [P, NCH])
        gate = sb("gate", [P, NCH])
        dstf = sb("dstf", [P, NCH])
        dsti = sb("dsti", [P, NCH], I32)
        srci = sb("srci", [P, NCH], I32)
        w1 = sb("w1", [P, 2, DH, F])
        w2 = sb("w2", [P, 2, FT, D])
        b2b = sb("b2b", [P, 2, D])
        bufr = sb("bufr", [P, 2, CT, D])
        bufT = sb("bufT", [P, 2, DH, CAP])
        hT = sb("hT", [P, FT, CAP])
        eo = sb("eo", [P, 2, CT, D])
        yg = qT[:].rearrange("p g n -> p (g n)").rearrange("p (c d) -> p c d", c=NCH)

        buf_d = nc.dram_tensor("dispatch_rows", [E * CAP + P, D], F32).ap()
        eo_d = nc.dram_tensor("expert_rows", [E * CAP, D], F32).ap()

        S = [psum(f"S{s}", [P, 3 * 512]) for s in range(B)]
        X = [psum(f"X{s}", [P, 512]) for s in range(B)]
        XT = [X[s][0:2 * H, 64:128].bitcast(BF16) for s in range(B)]

        s_cst = sem("s_cst")
        s_x = sems("s_x", 4)
        s_w = sem("s_w")
        s_small = sem("s_small")
        s_ctx = sem("s_ctx")
        s_zero = sem("s_zero")
        s_zsrc = sem("s_zsrc")
        s_vl = sem("s_vl")
        s_al = sem("s_al")
        s_cb = sem("s_cb")
        s_tg = sem("s_tg")
        s_xb = sem("s_xb")
        s_bob = sem("s_bob")
        s_smT = sem("s_smT")
        s_smc = sem("s_smc")
        s_cxT = sem("s_cxT")
        s_cxc = sem("s_cxc")
        s_kp = sem("s_kp")
        s_kc = sem("s_kc")
        s_vp = sem("s_vp")
        s_vc = sem("s_vc")
        s_sd = sem("s_sd")
        s_var = sem("s_var")
        s_xn = sems("s_xn")
        s_xt = sems("s_xt")
        s_xc = sems("s_xc")
        s_qp = sems("s_qp")
        s_qc = sems("s_qc")
        s_n2 = sems("s_n2")
        s_n2p = sems("s_n2p")
        s_n2t = sems("s_n2t")
        s_n2c = sems("s_n2c")
        s_lgp = sems("s_lgp")
        s_lgc = sems("s_lgc")
        s_ohb = sem("s_ohb")
        s_pos = sem("s_pos")
        s_sh = sem("s_sh")
        s_ex = sem("s_ex")
        s_idx = sem("s_idx")
        s_disp = sem("s_disp")
        s_w1 = sems("s_w1")
        s_w2 = sems("s_w2")
        s_b2 = sems("s_b2")
        s_buf = sems("s_buf")
        s_bt = sem("s_bt")
        s_btc = sem("s_btc")
        s_h = sem("s_h")
        s_ge = sem("s_ge")
        s_eo = sem("s_eo")
        s_flp = sem("s_flp")
        s_fls = sem("s_fls")
        s_flag = sem("s_flag")
        s_eoc = sem("s_eoc")
        s_eod = sems("s_eod")
        s_yg = sems("s_yg", 4)
        s_fin = sem("s_fin")
        s_out = sem("s_out")

        class Attention:

            def __init__(self, name, steps):
                self.general, self.steps = name == "g", steps
                self.score = sems(name + "_score")
                self.relu = sems(name + "_relu")
                self.mask = sems(name + "_mask")
                self.sum = sems(name + "_sum")
                self.step = sems(name + "_step")
                self.stT = sems(name + "_stT")
                self.stc = sems(name + "_stc")
                self.fin = sems(name + "_fin")
                self.res = sems(name + "_res")
                self.o = sems(name + "_o")
                self.oc = sems(name + "_oc")
                self.y = sems(name + "_y")
                self.x1 = sems(name + "_x1")
                self.st = sem(name + "_st")
                self.link = sem(name + "_link")
                self.SC = 2 * (steps + 1)
                self.MK = 2 * (steps - (not self.general))
                self.SM = steps + 1

            def masked(self, k):
                return self.general or k > 0

            def fine(self, k):
                return self.general or k >= COARSE

            def rows(self, k):
                return 2 * H if self.fine(k) else H

            def masks(self, k):
                return 2 * k if self.general else 2 * (k - 1)

            def loop(self, eng, body):
                if self.general:
                    with eng.Fori(0, self.steps) as k:
                        body(k)
                else:
                    for k in range(self.steps):
                        body(k)

        first = Attention("a", COARSE + FINE)
        general = Attention("g", GENERAL)

        def unless_converged(eng):
            eng.wait_ge(s_flag, 1)
            return eng.If(eng.value_load(flagi[0:1, 0:1], min_val=0, max_val=1) > 0)

        block = ctx.enter_context(nc.Block())

        @block.sync
        def _(sp):
            for s in range(2):
                sp.sem_inc(s_eod[s], 16)
            x_v = x_d.rearrange("(c p) d -> p c d", p=P)
            sp.dma_start(cst[:], cst_d).then_inc(s_cst, 16)
            sp.dma_start(cx[:], ctx_d.rearrange("b l d -> l b d")).then_inc(s_ctx, 16)
            for w_s, w_dr in ((wk, wk_d), (wv, wv_d), (wq, wq_d), (wo, wo_d)):
                sp.dma_start(w_s[:], w_dr.rearrange("(k p) n -> p k n", p=P)).then_inc(s_w, 16)
            for k in range(4):
                sp.dma_start(x[:, 4 * k:4 * k + 4, :], x_v[:, 4 * k:4 * k + 4, :]).then_inc(s_x[k], 16)
            sp.wait_ge(s_zsrc, 1)
            half = CAP * E // 2
            for k in range(2):
                sp.dma_start(buf_d[k * half:(k + 1) * half, :].rearrange("(p r) d -> p (r d)", p=P),
                             x1[:, 0:half // P, :].rearrange("p c d -> p (c d)")).then_inc(s_zero, 16)

            def load_w1(e, s):
                sp.dma_start(w1[:, s], w1_d[bass.ds(e, 1)].rearrange("a (k p) f -> p (a k) f", p=P)).then_inc(s_w1[s], 16)

            def load_w2(e, s):
                sp.dma_start(w2[:, s], w2_d[bass.ds(e, 1)].rearrange("a (k p) d -> p (a k) d", p=P)).then_inc(s_w2[s], 16)
                sp.dma_start(b2b[:, s, :], b2_d[bass.ds(e, 1), :].to_broadcast([P, D])).then_inc(s_b2[s], 16)

            def load_rows(e, s):
                sp.dma_start(bufr[:, s], buf_d[bass.ds(e * CAP, CAP), :].rearrange("(c p) d -> p c d", p=P)).then_inc(s_buf[s], 16)

            for s in range(2):
                load_w1(s, s)
                load_w2(s, s)
            sp.wait_ge(s_disp, 16 * NCH)
            for s in range(2):
                load_rows(s, s)

            def store(e, s):
                sp.wait_ge(s_eoc, CT * (e + 2))
                sp.dma_start(eo_d[bass.ds(e * CAP, CAP), :].rearrange("(c p) d -> p c d", p=P), eo[:, s]).then_inc(s_eod[s], 16)

            with sp.Fori(0, E // 2 - 1) as i:
                for s in range(2):
                    e = 2 * i + s
                    sp.wait_ge(s_bt, e + 1)
                    load_rows(e + 2, s)
                    sp.wait_ge(s_h, FT * (e + 1))
                    load_w1(e + 2, s)
                    store(e, s)
                    load_w2(e + 2, s)
            for s in range(2):
                store(E - 2 + s, s)
            for k in range(4):
                sp.wait_ge(s_fin, 4 * (k + 1))
                sp.dma_start(out_d.rearrange("(c p) d -> p c d", p=P)[:, 4 * k:4 * k + 4, :],
                             x1[:, 4 * k:4 * k + 4, :]).then_inc(s_out, 16)
            sp.wait_ge(s_out, 64)

        @block.gpsimd
        def _(gp):
            nc.gpsimd.memset(x1[:, 0:CAP * E // 2 // P, :], 0.0).then_inc(s_zsrc, 1)
            one = lambda ap, n: ap.rearrange("(a n) -> a n", a=1)
            for dst, src in ((rows[0:2, :], bq_d.rearrange("(g p) -> g p", p=P)),
                             (rows[2:4, :], bk_d.rearrange("(g p) -> g p", p=P)),
                             (bvr[:], one(bv_d, D)),
                             (bob[:], one(bo_d, D).to_broadcast([P, D])),
                             (gcol[:, 0:1], one(gx_d, 1).to_broadcast([P, 1])),
                             (gcol[:, 1:2], one(gf_d, 1).to_broadcast([P, 1])),
                             (rw[:], rw_d),
                             (b1r[:], b1_d.rearrange("e (f p) -> (e f) p", p=P))):
                gp.dma_start(dst, src).then_inc(s_small, 16)
            gp.wait_ge(s_bob, 1)
            with gp.Fori(0, CB) as i:
                for s in range(B):
                    c = i + CB * s
                    gp.wait_ge(s_xn[s], i + 1)
                    nc.gpsimd.tensor_tensor(x[:, bass.ds(c, 1), :], x[:, bass.ds(c, 1), :], bob[:].unsqueeze(1), ALU.add).then_inc(s_xb, 1)
            gp.wait_ge(s_zero, 32)
            for s in range(B):
                gp.wait_ge(s_n2p[s], CB + 1)
            gp.wait_ge(s_idx, 1)
            for c in range(NCH):
                gp.indirect_dma_start(out=buf_d, out_offset=bass.IndirectOffsetOnAxis(ap=dsti[:, c:c + 1], axis=0),
                                      in_=x[:, c, :], in_offset=None).then_inc(s_disp, 16)
            for s in range(2):
                gp.wait_ge(s_eod[s], 16 * (E // 2 + 1))
            for c in range(NCH):
                gp.indirect_dma_start(out=yg[:, c, :], out_offset=None, in_=eo_d,
                                      in_offset=bass.IndirectOffsetOnAxis(ap=srci[:, c:c + 1], axis=0)).then_inc(s_yg[c // 4], 16)

        @block.scalar
        def _(act):
            for s in range(B):
                act.sem_inc(s_qc[s], 1)
                act.sem_inc(s_n2p[s], 1)
                for q in (first, general):
                    act.sem_inc(q.relu[s], q.SC)
            act.sem_inc(s_ge, FT)
            act.wait_ge(s_small, 16 * 8)
            nc.scalar.activation(tg[:], gcol[:], ACT.Tanh).then_inc(s_tg, 1)
            act.wait_ge(s_cxT, 1)
            nc.scalar.copy(cxT[:].rearrange("p b k l -> p (b k l)"), X[1][:, 0:B * DH * L]).then_inc(s_cxc, 1)
            act.wait_ge(s_var, 1)
            nc.scalar.activation(sd[:], mv[:, :, 1], ACT.Sqrt, bias=eps[:, 0:1]).then_inc(s_sd, 1)
            with act.Fori(0, CB) as i:
                for s in range(B):
                    act.wait_ge(s_xt[s], i + 2)
                    nc.scalar.copy(xnT[:, s].rearrange("p k t -> p (k t)"), X[s][:, 0:D]).then_inc(s_xc[s], 1)
                for s in range(B):
                    act.wait_ge(s_qp[s], i + 1)
                    nc.scalar.activation(qT[:, 0, bass.ds(i * P + T * s, P)], X[s][:, D:D + P], ACT.Identity,
                                         bias=bqs[:, 0:1], scale=HD ** -0.5)
                    nc.scalar.activation(qT[:, 1, bass.ds(i * P + T * s, P)], X[s][:, D + P:D + 2 * P], ACT.Identity,
                                         bias=bqs[:, 1:2], scale=HD ** -0.5).then_inc(s_qc[s], 1)
            def attend(q):
                def relu(i, s, k, out):
                    for n, (a, b) in enumerate(PIECES):
                        act.wait_ge(q.score[s], q.SC * i + 2 * k + n + 1)
                        nc.scalar.activation(out[:, s, a * P:b * P], S[s][:, a * P:b * P], ACT.Relu).then_inc(q.relu[s], 1)

                with act.Fori(0, CB) as i:
                    def step(k):
                        for s in range(B):
                            relu(i, s, k, r16)
                    q.loop(act, step)
                    for s in range(B):
                        relu(i, s, q.steps, r32)
                    for s in range(B):
                        act.wait_ge(q.o[s], i + 1)
                        nc.scalar.copy(oT[:, s].rearrange("p g t -> p (g t)"), S[s][:, 512:512 + D]).then_inc(q.oc[s], 1)

            attend(first)
            with unless_converged(act):
                attend(general)
            act.wait_ge(s_var, 2)
            nc.scalar.activation(sd[:], mv[:, :, 1], ACT.Sqrt, bias=eps[:, 0:1]).then_inc(s_sd, 1)
            with act.Fori(0, CB) as i:
                for s in range(B):
                    act.wait_ge(s_n2t[s], i + 2)
                    nc.scalar.copy(xnT[:, s].rearrange("p k t -> p (k t)"), X[s][:, 0:D]).then_inc(s_n2c[s], 1)
                for s in range(B):
                    act.wait_ge(s_n2[s], i + 1)
                    nc.scalar.copy(x[:, bass.ds(i + CB * s, 1), :], xn[:, s:s + 1, :]).then_inc(s_n2p[s], 1)
            act.wait_ge(s_sh, 1)
            nc.scalar.activation(t3[:].rearrange("p c e -> p (c e)"), t3[:].rearrange("p c e -> p (c e)"), ACT.Exp).then_inc(s_ex, 1)
            with act.Fori(0, E) as e:
                for f in range(FT):
                    act.wait_ge(s_h, FT * e + f + 1)
                    nc.scalar.activation(hT[:, f, :], S[0][:, (f % 2) * 512:(f % 2) * 512 + CAP], ACT.Gelu,
                                         bias=b1T[:, bass.ds(FT * e + f, 1)]).then_inc(s_ge, 1)

        @block.vector
        def _(dve):
            for s in range(B):
                dve.sem_inc(s_lgc[s], 1)
                for q in (first, general):
                    dve.sem_inc(q.x1[s], 1)
                    dve.sem_inc(q.res[s], 1)
            dve.sem_inc(s_btc, DH)
            dve.sem_inc(s_eoc, CT)
            link = Link(dve, s_vl)
            dve.wait_ge(s_cst, 16)
            nc.vector.memset(eps[:], EPS)
            nc.vector.memset(off[:], 0.0)
            nc.vector.memset(KB[:], 0.0)
            nc.vector.memset(cxR[:], 0.0)
            nc.vector.tensor_copy(identb[:], ident)
            nc.vector.tensor_copy(trib[:], cst[:, C_TRI:C_TRI + P])
            nc.vector.tensor_copy(onesb[:], cst[:, C_ONE:C_ONE + P])
            nc.vector.tensor_copy(indb[:], ind32)
            nc.vector.tensor_copy(indh[:], ind32)
            link(nc.vector.tensor_copy(negb[:], cst[0:2 * H, C_NEG:C_NEG + W]))
            dve.wait_ge(s_smT, 1)
            nc.vector.tensor_copy(bcol[:], X[0][:, 0:4])
            nc.vector.tensor_copy(rwT[:].rearrange("p k e -> p (k e)"), X[0][:, 8:8 + DH * E])
            link(nc.vector.tensor_copy(b1T[:], X[0][:, 64:64 + E * FT]))
            nc.vector.tensor_scalar(bqs[:], bcol[:, 0:DH], HD ** -0.5, None, ALU.mult).then_inc(s_smc, 1)
            dve.wait_ge(s_tg, 1)
            nc.vector.tensor_scalar(bob[:], bob[:], tg[:, 0:1], None, ALU.mult).then_inc(s_bob, 1)
            dve.wait_ge(s_cxc, 1)
            for b in range(B):
                for k in range(DH):
                    last = nc.vector.tensor_copy(cxR[:, b, k, 0:HH * L].rearrange("p (h l) -> p h l", h=HH),
                                                 cxT[:, b, k, :].unsqueeze(1).to_broadcast([P, HH, L]))
            last.then_inc(s_cb, 1)
            dve.wait_ge(s_kp, 1)
            for n in range(B * DH):
                b, g = divmod(n, DH)
                ins = nc.vector.tensor_scalar(kT[:, b, g, :], X[0][:, n * P:n * P + L], bcol[:, DH + g:DH + g + 1], None,
                                              ALU.add, ALU.add, accum_out=ksum[:, n:n + 1])
            link(ins)
            link(nc.vector.tensor_scalar(ksum[:], ksum[:], 1.0 / L, None, ALU.mult))
            for n in range(B * DH):
                b, g = divmod(n, DH)
                ins = nc.vector.tensor_scalar(kT[:, b, g, :], kT[:, b, g, :], ksum[:, n:n + 1], None, ALU.subtract)
            link(ins)
            for n in range(B * DH):
                b, g = divmod(n, DH)
                ins = nc.vector.tensor_tensor(KB[:, b, g * KW:g * KW + HH * L].rearrange("p (h l) -> p h l", h=HH),
                                              kT[:, b, g, :].unsqueeze(1).to_broadcast([P, HH, L]),
                                              cst[:, C_HEAD:C_HEAD + HH].unsqueeze(2).to_broadcast([P, HH, L]), ALU.mult)
            ins.then_inc(s_kc, 1)
            for n in range(B * DH):
                b, g = divmod(n, DH)
                dve.wait_ge(s_vp, n + 1)
                nc.vector.tensor_tensor(VB[:, b, g * KT:(g + 1) * KT, :].rearrange("p t c -> p (t c)"), S[n % 2][:, 0:KW],
                                        cst[:, C_V:C_V + KW], ALU.mult).then_inc(s_vc, 1)

            def norm_scales():
                for c in range(NCH):
                    ins = nc.vector.bn_aggr(mv[:, c, :], stats[:, c, :])
                ins.then_inc(s_var, 1)

            for k in range(4):
                dve.wait_ge(s_x[k], 16)
                for c in range(4 * k, 4 * k + 4):
                    ins = nc.vector.bn_stats(stats[:, c, :], x[:, c, :])
            link(ins)
            norm_scales()
            dve.wait_ge(s_sd, 1)
            link(nc.vector.reciprocal(rs[:], sd[:]))
            with dve.Fori(0, CB) as i:
                for s in range(B):
                    c = i + CB * s
                    dve.wait_ge(s_xt[s], i + 1)
                    nc.vector.tensor_scalar(xn[:, s:s + 1, :], x[:, bass.ds(c, 1), :], mv[:, bass.ds(c, 1), 0:1].squeeze(2),
                                            rs[:, bass.ds(c, 1)], ALU.subtract, ALU.mult).then_inc(s_xn[s], 1)

            def attend(q):
                link = Link(dve, q.link)
                fine_links, coarse_links, guess_links, end_links = 4, 2, 1, 2
                per_chunk = B * (end_links + (q.steps * fine_links if q.general else
                                              guess_links + (COARSE - 1) * coarse_links + FINE * fine_links))

                def step_of(i, s, k, before):
                    link.at(per_chunk * i + before)
                    if q.masked(k):
                        for n, (a, b) in enumerate(PIECES):
                            cols = slice(a * P, b * P)
                            dve.wait_ge(q.relu[s], q.SC * (i + 1) + 2 * k + n + 1)
                            ins = nc.vector.tensor_scalar(msk[:, s, cols], r16[:, s, cols], 0.0, None, ALU.is_gt)
                            if q.fine(k):
                                ins = nc.vector.scalar_tensor_tensor(rlo[:, s, cols], S[s][:, cols], 0.0, r16[:, s, cols],
                                                                     ALU.max, ALU.subtract)
                            ins.then_inc(q.mask[s], 1)
                    dve.wait_ge(q.sum[s], q.SM * i + k + 1)
                    total, count = X[s][:, 0:H], X[s][:, H:2 * H]
                    if not q.masked(k):
                        link(nc.vector.tensor_scalar(step[:, s, :], total, GUESS[0], GUESS[1], ALU.mult, ALU.add))
                        nc.vector.tensor_scalar(parts[:, s, 0:H], step[:, s, :], GUESS[2], None, ALU.min).then_inc(q.step[s], 1)
                    else:
                        link(nc.vector.tensor_scalar(cnt[:, s, :], count, 1.0, None, ALU.max))
                        link(nc.vector.reciprocal(cnt[:, s, :], cnt[:, s, :]))
                        if not q.fine(k):
                            nc.vector.scalar_tensor_tensor(parts[:, s, 0:H], total, -1.0, cnt[:, s, :],
                                                           ALU.add, ALU.mult).then_inc(q.step[s], 1)
                        else:
                            link(nc.vector.scalar_tensor_tensor(step[:, s, :], total, -1.0, cnt[:, s, :], ALU.add, ALU.mult))
                            link(nc.vector.tensor_copy(parts[:, s, 0:H], step[:, s, :]))
                            nc.vector.tensor_tensor(parts[:, s, H:2 * H], step[:, s, :], parts[:, s, 0:H],
                                                    ALU.subtract).then_inc(q.step[s], 1)
                    dve.wait_ge(q.stT[s], q.steps * i + k + 1)
                    nc.vector.tensor_copy(partsT[0:q.rows(k), s, :], XT[s][0:q.rows(k), :]).then_inc(q.stc[s], 1)
                    return link.n

                with dve.Fori(0, CB) as i:
                    if q.general:
                        with dve.Fori(0, q.steps) as k:
                            for s in range(B):
                                assert step_of(i, s, k, B * fine_links * k + fine_links * s) == fine_links
                        before = B * fine_links * q.steps
                    else:
                        before = 0
                        for k in range(q.steps):
                            for s in range(B):
                                before += step_of(i, s, k, before)
                    link.at(per_chunk * i + before)
                    for s in range(B):
                        dve.wait_ge(q.relu[s], q.SC * (i + 2))
                        nc.vector.tensor_copy(r16[:, s, :], r32[:, s, :]).then_inc(q.fin[s], 1)
                    for s in range(B):
                        dve.wait_ge(q.fin[s], 2 * i + 1)
                        nc.vector.tensor_tensor(rlo[:, s, :], r32[:, s, :], r16[:, s, :], ALU.subtract).then_inc(q.fin[s], 1)
                    for s in range(B):
                        c = i + CB * s
                        dve.wait_ge(q.y[s], i + 1)
                        if not q.general:
                            dve.wait_ge(s_xb, B * i + s + 1)
                        nc.vector.scalar_tensor_tensor(x1[:, bass.ds(c, 1), :], S[s][:, 1024:1024 + D].unsqueeze(1), tg[:, 0:1],
                                                       x[:, bass.ds(c, 1), :], ALU.mult, ALU.add).then_inc(q.x1[s], 1)
                    for s in range(B):
                        dve.wait_ge(q.sum[s], q.SM * (i + 1))
                        nc.vector.tensor_scalar(step[:, s, :], X[s][:, 0:H], -1.0, None, ALU.add).then_inc(q.res[s], 1)
                    for s in range(B):
                        c = i + CB * s
                        dve.wait_ge(q.x1[s], i + 2)
                        nc.vector.bn_stats(stats[:, bass.ds(c, 1), :].squeeze(1), x1[:, bass.ds(c, 1), :].squeeze(1)).then_inc(q.st, 1)
                    for s in range(B):
                        dve.wait_ge(q.res[s], i + 2)
                        link(nc.vector.tensor_tensor(rest[:, s, :], step[:, s, :], step[:, s, :], ALU.mult))
                        link(nc.vector.tensor_tensor(off[:, s, :], off[:, s, :], rest[:, s, :], ALU.max))
                    assert q.general or link.n + before == per_chunk
                dve.wait_ge(q.st, NCH)

            dve.wait_ge(s_zero, 32)
            attend(first)
            link(nc.vector.tensor_reduce(out=flag[:, 0:1], in_=off[:].rearrange("p b h -> p (b h)"), axis=AX_X, op=ALU.max))
            nc.vector.tensor_scalar(flag[:, 1:2], flag[:, 0:1], LIMIT, None, ALU.is_gt).then_inc(s_flp, 1)
            dve.wait_ge(s_fls, 1)
            nc.vector.tensor_scalar(flagi[:], X[0][0:1, 0:1], 1.0, None, ALU.min).then_inc(s_flag, 1)
            with unless_converged(dve):
                attend(general)
            norm_scales()
            dve.wait_ge(s_sd, 2)
            link(nc.vector.reciprocal(rs[:], sd[:]))
            with dve.Fori(0, CB) as i:
                for s in range(B):
                    c = i + CB * s
                    dve.wait_ge(s_n2t[s], i + 1)
                    dve.wait_ge(s_n2p[s], i + 1)
                    nc.vector.tensor_scalar(xn[:, s:s + 1, :], x1[:, bass.ds(c, 1), :], mv[:, bass.ds(c, 1), 0:1].squeeze(2),
                                            rs[:, bass.ds(c, 1)], ALU.subtract, ALU.mult).then_inc(s_n2[s], 1)
                for s in range(B):
                    dve.wait_ge(s_lgp[s], i + 1)
                    nc.vector.tensor_copy(lg[:, bass.ds(i + CB * s, 1), :], X[s][:, D:D + E].unsqueeze(1)).then_inc(s_lgc[s], 1)
            for s in range(B):
                dve.wait_ge(s_lgc[s], CB + 1)
            wide = lambda ap: ap.unsqueeze(2).to_broadcast([P, NCH, E])
            each = lambda c: cst[:, c:c + E].unsqueeze(1).to_broadcast([P, NCH, E])
            link(nc.vector.tensor_reduce(out=lmax[:], in_=lg[:], axis=AX_X, op=ALU.max))
            nc.vector.tensor_tensor(t3[:], lg[:], wide(lmax[:]), ALU.subtract).then_inc(s_sh, 1)
            link(nc.vector.tensor_tensor(oh[:], lg[:], wide(lmax[:]), ALU.is_equal))
            link(nc.vector.tensor_tensor(oh[:], oh[:], each(C_REV), ALU.mult))
            link(nc.vector.tensor_reduce(out=t2[:], in_=oh[:], axis=AX_X, op=ALU.max))
            link(nc.vector.tensor_tensor(oh[:], wide(t2[:]), each(C_REV), ALU.is_equal))
            nc.vector.tensor_copy(ohb[:], oh[:]).then_inc(s_ohb, 1)
            dve.wait_ge(s_ex, 1)
            link(nc.vector.tensor_reduce(out=t2[:], in_=t3[:], axis=AX_X, op=ALU.add))
            link(nc.vector.reciprocal(gate[:], t2[:]))
            link(nc.vector.tensor_scalar(gate[:], gate[:], tg[:, 1:2], None, ALU.mult))
            link(nc.vector.tensor_tensor(t3[:], oh[:], each(C_BASE), ALU.mult))
            link(nc.vector.tensor_reduce(out=base[:], in_=t3[:], axis=AX_X, op=ALU.add))
            dve.wait_ge(s_pos, 1)
            link(nc.vector.tensor_tensor(t3[:], X[0][:, 0:NCH * E].rearrange("p (c e) -> p c e", e=E), oh[:], ALU.mult))
            link(nc.vector.tensor_reduce(out=pos[:], in_=t3[:], axis=AX_X, op=ALU.add))
            link(nc.vector.tensor_scalar(kept[:], pos[:], float(CAP), None, ALU.is_lt))
            link(nc.vector.tensor_tensor(gate[:], gate[:], kept[:], ALU.mult))
            link(nc.vector.tensor_tensor(dstf[:], base[:], pos[:], ALU.add))
            link(nc.vector.tensor_scalar(dstf[:], dstf[:], cst[:, C_ROW:C_ROW + 1], None, ALU.subtract))
            link(nc.vector.tensor_tensor(dstf[:], dstf[:], kept[:], ALU.mult))
            link(nc.vector.tensor_scalar(dsti[:], dstf[:], cst[:, C_ROW:C_ROW + 1], None, ALU.add))
            link(nc.vector.tensor_scalar(pos[:], pos[:], float(CAP - 1), None, ALU.min))
            nc.vector.tensor_tensor(srci[:], base[:], pos[:], ALU.add).then_inc(s_idx, 1)
            with dve.Fori(0, E // 2) as i:
                for s in range(2):
                    e = 2 * i + s
                    dve.wait_ge(s_bt, e + 1)
                    for k in range(DH):
                        nc.vector.tensor_copy(bufT[:, s, k, :], X[k][:, 0:CAP]).then_inc(s_btc, 1)
                    dve.wait_ge(s_b2[s], 16 * i + 16)
                    dve.wait_ge(s_eod[s], 16 * (i + 1))
                    for t in range(CT):
                        dve.wait_ge(s_eo, CT * e + t + 1)
                        nc.vector.tensor_tensor(eo[:, s, t, :], S[1][:, 512 * t:512 * t + D], b2b[:, s, :], ALU.add).then_inc(s_eoc, 1)
            for k in range(4):
                dve.wait_ge(s_yg[k], 64)
                for c in range(4 * k, 4 * k + 4):
                    nc.vector.scalar_tensor_tensor(x1[:, c, :], yg[:, c, :], gate[:, c:c + 1], x1[:, c, :],
                                                   ALU.mult, ALU.add).then_inc(s_fin, 1)

        @block.tensor
        def _(pe):
            mm = nc.tensor.matmul

            def acc(out, lhsT, rhs, first):
                return mm(out, lhsT, rhs, start=first, stop=True, skip_group_check=True)

            for s in range(B):
                pe.sem_inc(s_xt[s], 1)
                pe.sem_inc(s_n2t[s], 1)
            pe.wait_ge(s_cst, 16)
            pe.wait_ge(s_ctx, 16)
            for b in range(B):
                for k in range(DH):
                    n = b * DH + k
                    last = nc.tensor.transpose(X[1][:, n * L:(n + 1) * L], cx[:, b, k * P:(k + 1) * P], ident[0:L, 0:L])
            last.then_inc(s_cxT, 1)
            pe.wait_ge(s_small, 16 * 8)
            nc.tensor.transpose(X[0][:, 0:4], rows[0:4, :], ident[0:4, 0:4])
            for k in range(DH):
                nc.tensor.transpose(X[0][:, 8 + k * E:8 + (k + 1) * E], rw[:, k * P:(k + 1) * P], ident[0:E, 0:E])
            nc.tensor.transpose(X[0][:, 64:64 + E * FT], b1r[:], ident[0:E * FT, 0:E * FT]).then_inc(s_smT, 1)
            pe.wait_ge(s_smc, 1)
            pe.wait_ge(s_cxc, 1)
            pe.wait_ge(s_w, 64)
            for n in range(B * DH):
                b, g = divmod(n, DH)
                for k in range(DH):
                    last = mm(X[0][:, n * P:n * P + L], wk[:, k, g * P:(g + 1) * P], cxT[:, b, k, :], start=k == 0, stop=k == DH - 1)
            last.then_inc(s_kp, 1)
            pe.wait_ge(s_cb, 1)
            for n in range(B * DH):
                b, g = divmod(n, DH)
                if n >= 2:
                    pe.wait_ge(s_vc, n - 1)
                for t in range(KT):
                    out = S[n % 2][:, t * P:(t + 1) * P]
                    for k in range(DH):
                        mm(out, cxR[:, b, k, t * P:(t + 1) * P], wv[:, k, g * P:(g + 1) * P], start=k == 0, stop=False)
                    last = mm(out, ones_row, bvr[:, g * P:(g + 1) * P], start=False, stop=True)
                last.then_inc(s_vp, 1)
            pe.wait_ge(s_kc, 1)
            with pe.Fori(0, CB) as i:
                for s in range(B):
                    pe.wait_ge(s_xn[s], i + 1)
                    pe.wait_ge(s_qc[s], i + 1)
                    for k in range(DH):
                        last = nc.tensor.transpose(X[s][:, k * P:(k + 1) * P], xn[:, s, k * P:(k + 1) * P], ident)
                    last.then_inc(s_xt[s], 1)
                for s in range(B):
                    pe.wait_ge(s_xc[s], i + 1)
                    for g in range(DH):
                        for k in range(DH):
                            last = mm(X[s][:, D + g * P:D + (g + 1) * P], wq[:, k, g * P:(g + 1) * P], xnT[:, s, k, :],
                                      start=k == 0, stop=k == DH - 1)
                    last.then_inc(s_qp[s], 1)
            for s in range(B):
                pe.wait_ge(s_qc[s], CB + 1)
            pe.wait_ge(s_vc, B * DH)

            def attend(q):
                def scores(i, s):
                    pe.wait_ge(q.relu[s], q.SC * (i + 1))
                    pe.wait_ge(q.x1[s], i + 1)
                    for a, b in PIECES:
                        for t in range(a, b):
                            last = acc(S[s][:, t * P:(t + 1) * P], KB[:, s, t * P:(t + 1) * P],
                                       qT[:, t // KT, bass.ds(i * P + T * s, P)], t % 4 == 0)
                        last.then_inc(q.score[s], 1)

                def add(out, s, part, ind, n, first=False):
                    for t in range(*PIECES[n]):
                        last = acc(out, part[:, s, t * P:(t + 1) * P], ind[:, t, :], first and t == 0)
                    return last

                def sums(i, s, k):
                    if q.general or k == 0:
                        pe.wait_ge(q.res[s], i + 1)
                    for n in range(2):
                        pe.wait_ge(q.relu[s], q.SC * (i + 1) + 2 * k + n + 1)
                        last = add(X[s][:, 0:H], s, r16, indb, n, n == 0)
                        if q.masked(k):
                            pe.wait_ge(q.mask[s], q.MK * i + q.masks(k) + n + 1)
                            last = add(X[s][:, H:2 * H], s, msk, indb, n)
                        if q.fine(k):
                            last = add(X[s][:, 0:H], s, rlo, indh, n)
                    last.then_inc(q.sum[s], 1)

                def result_sums(i, s):
                    pe.wait_ge(q.fin[s], 2 * i + 2)
                    for n in range(2):
                        add(X[s][:, 0:H], s, r16, indb, n, n == 0)
                        last = add(X[s][:, 0:H], s, rlo, indh, n)
                    last.then_inc(q.sum[s], 1)

                def turn(i, s, k):
                    pe.wait_ge(q.step[s], q.steps * i + k + 1)
                    nc.tensor.transpose(XT[s][0:q.rows(k), :], parts[:, s, 0:q.rows(k)], identb[:]).then_inc(q.stT[s], 1)

                def move(i, s, k):
                    pe.wait_ge(q.stc[s], q.steps * i + k + 1)
                    for a, b in PIECES:
                        for t in range(a, b):
                            last = acc(S[s][:, t * P:(t + 1) * P], negb[0:q.rows(k), t * P:(t + 1) * P],
                                       partsT[0:q.rows(k), s, :], False)
                        last.then_inc(q.score[s], 1)

                with pe.Fori(0, CB) as i:
                    for s in range(B):
                        scores(i, s)

                    def step(k):
                        sums(i, 0, k)
                        turn(i, 0, k)
                        sums(i, 1, k)
                        move(i, 0, k)
                        turn(i, 1, k)
                        move(i, 1, k)
                    q.loop(pe, step)
                    for s in range(B):
                        pe.wait_ge(q.relu[s], q.SC * (i + 2))
                        for t in range(NT):
                            g = t // KT
                            last = acc(S[s][:, 512 + g * P:512 + (g + 1) * P], VB[:, s, t, :], r32[:, s, t * P:(t + 1) * P], t == 0)
                        last.then_inc(q.o[s], 1)
                    for s in range(B):
                        result_sums(i, s)
                    for s in range(B):
                        pe.wait_ge(q.oc[s], i + 1)
                        for g in range(DH):
                            last = mm(S[s][:, 1024:1024 + D], oT[:, s, g, :], wo[:, g, :], start=g == 0, stop=g == DH - 1)
                        last.then_inc(q.y[s], 1)
                for s in range(B):
                    pe.wait_ge(q.x1[s], CB + 1)
                    pe.wait_ge(q.res[s], CB + 1)

            attend(first)
            pe.wait_ge(s_flp, 1)
            mm(X[0][:, 0:1], cst[:, C_ONE:C_ONE + P], flag[:, 1:2], start=True, stop=True).then_inc(s_fls, 1)
            with unless_converged(pe):
                attend(general)
            with pe.Fori(0, CB) as i:
                for s in range(B):
                    pe.wait_ge(s_n2[s], i + 1)
                    pe.wait_ge(s_lgc[s], i + 1)
                    for k in range(DH):
                        last = nc.tensor.transpose(X[s][:, k * P:(k + 1) * P], xn[:, s, k * P:(k + 1) * P], ident)
                    last.then_inc(s_n2t[s], 1)
                for s in range(B):
                    pe.wait_ge(s_n2c[s], i + 1)
                    for k in range(DH):
                        last = mm(X[s][:, D:D + E], xnT[:, s, k, :], rwT[:, k, :], start=k == 0, stop=k == DH - 1)
                    last.then_inc(s_lgp[s], 1)
            pe.wait_ge(s_ohb, 1)
            for s in range(B):
                pe.wait_ge(s_lgc[s], CB + 1)
            acc(X[0][:, 0:NCH * E], trib[:], ohb[:].rearrange("p c e -> p (c e)"), True)
            for c in range(1, NCH):
                last = acc(X[0][:, c * E:NCH * E].rearrange("p (c e) -> p c e", e=E), onesb[:],
                           ohb[:, c - 1:c, :].to_broadcast([P, NCH - c, E]), False)
            last.then_inc(s_pos, 1)
            pe.wait_ge(s_idx, 1)

            def turn_rows(i, s):
                pe.wait_ge(s_buf[s], 16 * i + 16)
                pe.wait_ge(s_btc, DH * (2 * i + s + 1))
                for k in range(DH):
                    for t in range(CT):
                        last = nc.tensor.transpose(X[k][:, t * P:(t + 1) * P], bufr[:, s, t, k * P:(k + 1) * P], ident)
                last.then_inc(s_bt, 1)

            def up(i, s, f):
                e = 2 * i + s
                if f == 0:
                    pe.wait_ge(s_w1[s], 16 * i + 16)
                    pe.wait_ge(s_btc, DH * (e + 2))
                if f >= 2:
                    pe.wait_ge(s_ge, FT * (e + 1) + f - 1)
                else:
                    pe.wait_ge(s_ge, FT * (e + 1))
                for k in range(DH):
                    last = mm(S[0][:, (f % 2) * 512:(f % 2) * 512 + CAP], w1[:, s, k, f * P:(f + 1) * P], bufT[:, s, k, :],
                              start=k == 0, stop=k == DH - 1)
                last.then_inc(s_h, 1)

            def down(i, s, f):
                e = 2 * i + s
                if f == 0:
                    pe.wait_ge(s_w2[s], 16 * i + 16)
                    pe.wait_ge(s_eoc, CT * (e + 1))
                pe.wait_ge(s_ge, FT * (e + 1) + f + 1)
                for t in range(CT):
                    last = mm(S[1][:, 512 * t:512 * t + D], hT[:, f, t * P:(t + 1) * P], w2[:, s, f, :],
                              start=f == 0, stop=f == FT - 1)
                    if f == FT - 1:
                        last.then_inc(s_eo, 1)

            def expert(i, s, more):
                up(i, s, 0)
                for f in range(1, FT):
                    up(i, s, f)
                    down(i, s, f - 1)
                if more:
                    turn_rows(i + s, 1 - s)
                down(i, s, FT - 1)

            turn_rows(0, 0)
            with pe.Fori(0, E // 2 - 1) as i:
                for s in range(2):
                    expert(i, s, True)
            expert(E // 2 - 1, 0, True)
            expert(E // 2 - 1, 1, False)


_INPUTS = {
    "x": "x", "ctx_1024": "ctx", "g_xattn": "gx", "g_ffn": "gf",
    "L0_xattn_Wq": "wq", "L0_xattn_bq": "bq", "L0_xattn_Wk": "wk", "L0_xattn_bk": "bk",
    "L0_xattn_Wv": "wv", "L0_xattn_bv": "bv", "L0_xattn_Wo": "wo", "L0_xattn_bo": "bo",
    "L0_ffn_router_w": "rw", "L0_ffn_w1": "w1", "L0_ffn_b1": "b1", "L0_ffn_w2": "w2", "L0_ffn_b2": "b2",
}


def kernel(**inputs):
    import concourse.bacc as bacc
    from concourse.bass_utils import run_bass_kernel_spmd

    nc = bacc.Bacc("TRN2", target_bir_lowering=False, num_devices=1)
    arrays, args = {}, []
    for name, short in _INPUTS.items():
        a = np.ascontiguousarray(inputs[name])
        if name == "x":
            a = a.reshape(N, D)
        arrays[f"{short}_dram"] = a
    arrays["cst_dram"] = constants()
    for name, a in arrays.items():
        args.append(nc.dram_tensor(name, a.shape, mybir.dt.from_np(a.dtype), kind="ExternalInput").ap())
    args.append(nc.dram_tensor("out_dram", (N, D), F32, kind="ExternalOutput").ap())
    flamingo_layer(nc, *args)
    r = run_bass_kernel_spmd(nc, [arrays], core_ids=[0])
    return r.results[0]["out_dram"].reshape(B, T, D)
```

```python
from contextlib import ExitStack

import numpy as np

import concourse.bass as bass
from concourse import mybir

ALU = mybir.AluOpType
ACT = mybir.ActivationFunctionType
F32 = mybir.dt.float32
BF16 = mybir.dt.bfloat16
FP16 = mybir.dt.float16
I32 = mybir.dt.int32
AX_X = mybir.AxisListType.X

P = 128
B = 2
T = 1024
N = B * T
D = 256
DH = D // P
H = 16
HD = D // H
HH = H // DH
L = 77
E = 8
F = 1024
FT = F // P
CAP = -(-3 * N // (2 * E))
CT = CAP // P
NCH = N // P
CB = T // P
KT = -(-HH * L // P)
KW = KT * P
W = DH * KW
NT = DH * KT
EPS = 1e-5
PIECES = ((0, 4), (4, NT))

LOW_AT = ((), (), (0,), (1, 2), (3,), (4,), (5, 6), (7,))
TURN = 4
WS = 64.0
COARSE = 4
FINE = 2
GENERAL = 32
LIMIT = 1e-10
WARM = (5, 4)
GUESS = (0.0497, -0.1, 0.22)

C_ID = 0
C_TRI = C_ID + P
C_ONE = C_TRI + P
C_HEAD = C_ONE + P
C_IND = C_HEAD + HH
C_IOTA = C_IND + NT * H
C_REV = C_IOTA + E
C_BASE = C_REV + E
C_ROW = C_BASE + E
C_ALL = C_ROW + 1


def constants():
    c = np.zeros((P, C_ALL), np.float32)
    neg = np.zeros((2 * H, W), np.float32)
    r = np.arange(P)
    c[:, C_ID:C_ID + P] = np.eye(P)
    c[:, C_TRI:C_TRI + P] = r[:, None] < r[None, :]
    c[:, C_ONE:C_ONE + P] = 1
    c[:, C_HEAD:C_HEAD + HH] = r[:, None] // HD == np.arange(HH)
    hk = np.arange(KW)
    head = np.where(hk < HH * L, hk // L, -1)
    sel = (np.arange(L)[:, None] == np.where(head >= 0, hk % L, -1)).astype(np.float32)
    for g in range(DH):
        hg = np.where(head >= 0, head + g * HH, -1)
        ind = hg.reshape(KT, P).T[:, :, None] == np.arange(H)
        c[:, C_IND + g * KT * H:C_IND + (g + 1) * KT * H] = ind.reshape(P, KT * H)
        neg[:, g * KW:(g + 1) * KW] = np.where(hg[None, :] == np.arange(2 * H)[:, None] % H, -1, 0)
    c[:, C_IOTA:C_IOTA + E] = np.arange(E)
    c[:, C_REV:C_REV + E] = E - np.arange(E)
    c[:, C_BASE:C_BASE + E] = np.arange(E) * CAP
    c[:, C_ROW] = E * CAP + r
    return {"cst": c, "sel": sel, "neg": neg}


class Link:

    def __init__(self, eng, sem):
        self.eng, self.sem, self.n, self.base = eng, sem, 0, 0

    def at(self, base):
        self.base, self.n = base, 0

    def __call__(self, ins):
        self.n += 1
        ins.then_inc(self.sem, 1)
        self.eng.wait_ge(self.sem, self.base + self.n)


def flamingo_layer(nc, x_d, ctx_d, gx_d, gf_d, wq_d, bq_d, wk_d, bk_d, wv_d, bv_d, wo_d, bo_d,
                   rw_d, w1_d, b1_d, w2_d, b2_d, cst_d, sel_d, neg_d, out_d):
    with ExitStack() as ctx:
        def sb(name, shape, dt=F32):
            return ctx.enter_context(nc.sbuf_tensor(name, shape, dt))

        def psum(name, shape, dt=F32):
            return ctx.enter_context(nc.psum_tensor(name, shape, dt))

        def sem(name):
            return ctx.enter_context(nc.semaphore(name))

        def sems(name, n=B):
            return [sem(f"{name}{i}") for i in range(n)]

        cst = sb("cst", [P, C_ALL])
        ident = cst[:, C_ID:C_ID + P]
        identb = sb("identb", [P, P], BF16)
        trib = sb("trib", [P, P], BF16)
        onesb = sb("onesb", [P, P], BF16)
        ones_row = cst[0:1, C_ONE:C_ONE + P]
        ind32 = cst[:, C_IND:C_IND + NT * H].rearrange("p (t h) -> p t h", t=NT)
        indb = sb("indb", [P, NT, H], BF16)
        indh = sb("indh", [P, NT, H], FP16)
        negb = sb("negb", [P, W], BF16)
        nega = sb("nega", [P, W], BF16)
        wq = sb("wq", [P, DH, D])
        wk = sb("wk", [P, DH, D])
        wv = sb("wv", [P, DH, D])
        wo = sb("wo", [P, DH, D])
        rows = sb("rows", [8, P])
        bcol = sb("bcol", [P, 4])
        bqs = sb("bqs", [P, DH])
        bvr = sb("bvr", [1, D])
        bob = sb("bob", [P, D])
        gcol = sb("gcol", [P, 2])
        tg = sb("tg", [P, 2])
        eps = sb("eps", [P, 1])
        rw = sb("rw", [E, D])
        rwT = sb("rwT", [P, DH, E])
        b1r = sb("b1r", [E * FT, P])
        b1T = sb("b1T", [P, E * FT])
        cx = sb("cx", [L, B, D])
        cxT = sb("cxT", [P, B, DH, L])
        sel = sb("sel", [L, KW])
        neg32 = sb("neg32", [2 * H, W])
        vs = sb("vs", [L, B, D])
        kT = sb("kT", [P, B, DH, L])
        ksum = sb("ksum", [P, B * DH])
        KB = sb("KB", [P, B, W])
        VB = sb("VB", [P, B, NT, P])
        x = sb("x", [P, NCH, D])
        x1 = sb("x1", [P, NCH, D])
        stats = sb("stats", [P, NCH, 6])
        mv = sb("mv", [P, NCH, 2])
        sd = sb("sd", [P, NCH])
        rs = sb("rs", [P, NCH])
        xn = sb("xn", [P, B, D])
        xnT = sb("xnT", [P, B, DH, P])
        qT = sb("qT", [P, DH, N])
        r16 = sb("r16", [P, B, W], BF16)
        msk = sb("msk", [P, B, W], BF16)
        rlo = sb("rlo", [P, B, W], FP16)
        r32 = sb("r32", [P, B, W])
        flag = sb("flag", [P, 2])
        flagi = sb("flagi", [1, 1], I32)
        off = sb("off", [P, B, H])
        cnt = sb("cnt", [P, B, H])
        step = sb("step", [P, B, H])
        rest = sb("rest", [P, B, H])
        parts = sb("parts", [P, B, 2 * H], BF16)
        partsT = sb("partsT", [P, B, P], BF16)
        oT = sb("oT", [P, B, DH, P])
        lg = sb("lg", [P, NCH, E])
        lmax = sb("lmax", [P, NCH])
        oh = sb("oh", [P, NCH, E])
        ohb = sb("ohb", [P, NCH, E], BF16)
        t3 = sb("t3", [P, NCH, E])
        t2 = sb("t2", [P, NCH])
        pos = sb("pos", [P, NCH])
        base = sb("base", [P, NCH])
        kept = sb("kept", [P, NCH])
        gate = sb("gate", [P, NCH])
        dstf = sb("dstf", [P, NCH])
        dsti = sb("dsti", [P, NCH], I32)
        srci = sb("srci", [P, NCH], I32)
        w1 = sb("w1", [P, 2, DH, F])
        w2 = sb("w2", [P, 2, FT, D])
        b2b = sb("b2b", [P, 2, D])
        bufr = sb("bufr", [P, 2, CT, D])
        xh = sb("xh", [P, 2, DH, CAP], FP16)
        xl = sb("xl", [P, 2, DH, CAP], FP16)
        hT = sb("hT", [P, 2, CAP])
        q_free = qT[:].rearrange("p g n -> p (g n)")
        HALF = FT * CAP // 2
        hh, hl = (q_free[:, n * HALF:(n + 1) * HALF].bitcast(FP16).rearrange("p (f c) -> p f c", f=FT) for n in range(2))

        def as_weights(buf):
            flat = buf[:].rearrange("p a b -> p (a b)") if len(buf.shape) == 3 else buf[:].rearrange("p a b c -> p (a b c)")
            return flat[:, 0:DH * F].bitcast(FP16).rearrange("p (s q c) -> p s q c", s=2, q=4)

        w1h, w1l, w2h = as_weights(KB), as_weights(VB), as_weights(r32)
        scale = sb("scale", [P, DH * F // 4])
        warm_up = sb("warm_up", [P, 1])
        b1e = sb("b1e", [P, 2, FT])
        w2l = sb("w2l", [P, 2, 4, DH * F // 4], FP16)
        w1q = w1[:].rearrange("p s k f -> p s (k f)").rearrange("p s (q c) -> p s q c", q=4)
        w2q = w2[:].rearrange("p s f d -> p s (f d)").rearrange("p s (q c) -> p s q c", q=4)
        QUARTERS = [(w1q, w1h, w1l, q) for q in range(4)] + [(w2q, w2h, w2l, q) for q in range(4)]
        NQ = len(QUARTERS)

        def w1_part(part, s, k, f):
            per = F // 2 // P
            return part[:, s, 2 * k + f // per, f % per * P:(f % per + 1) * P]

        def w2_part(part, s, f):
            return part[:, s, f // 2, f % 2 * D:(f % 2 + 1) * D]
        eo = sb("eo", [P, 2, CT, D])
        yg = qT[:].rearrange("p g n -> p (g n)").rearrange("p (c d) -> p c d", c=NCH)

        buf_d = nc.dram_tensor("dispatch_rows", [E * CAP + P, D], F32).ap()
        eo_d = nc.dram_tensor("expert_rows", [E * CAP, D], F32).ap()

        S = [psum(f"S{s}", [P, 3 * 512]) for s in range(B)]
        X = [psum(f"X{s}", [P, 512]) for s in range(B)]
        XT = [X[s][0:2 * H, 64:128].bitcast(BF16) for s in range(B)]

        s_cst = sem("s_cst")
        s_x = sems("s_x", 4)
        s_wk = sem("s_wk")
        s_wv = sem("s_wv")
        s_w = sem("s_w")
        s_sel = sem("s_sel")
        s_neg = sem("s_neg")
        s_kb = sem("s_kb")
        s_small = sem("s_small")
        s_ctx = sem("s_ctx")
        s_zero = sem("s_zero")
        s_zsrc = sem("s_zsrc")
        s_setup = sem("s_setup")
        s_vs = sem("s_vs")
        s_tg = sem("s_tg")
        s_xb = sem("s_xb")
        s_bob = sem("s_bob")
        s_smT = sem("s_smT")
        s_smc = sem("s_smc")
        s_cxT = sem("s_cxT")
        s_cxc = sem("s_cxc")
        s_kp = sem("s_kp")
        s_kc = sem("s_kc")
        s_vp = sem("s_vp")
        s_sp = sem("s_sp")
        s_vc = sem("s_vc")
        s_sd = sem("s_sd")
        s_var = sem("s_var")
        s_xn = sems("s_xn")
        s_xt = sems("s_xt")
        s_xc = sems("s_xc")
        s_qp = sems("s_qp")
        s_qc = sems("s_qc")
        s_n2 = sems("s_n2")
        s_n2p = sems("s_n2p")
        s_n2t = sems("s_n2t")
        s_n2c = sems("s_n2c")
        s_lgp = sems("s_lgp")
        s_lgc = sems("s_lgc")
        s_ohb = sem("s_ohb")
        s_pos = sem("s_pos")
        s_sh = sem("s_sh")
        s_ex = sem("s_ex")
        s_idx = sem("s_idx")
        s_disp = sem("s_disp")
        s_w1 = sems("s_w1")
        s_w2 = sems("s_w2")
        s_b2 = sems("s_b2")
        s_buf = sems("s_buf")
        s_bt = sem("s_bt")
        s_btc = sem("s_btc")
        s_h = sem("s_h")
        s_scale = sem("s_scale")
        s_b1e = sem("s_b1e")
        s_hl = sem("s_hl")
        s_bth = sem("s_bth")
        s_wh = sem("s_wh")
        s_wl = sem("s_wl")
        s_ge = sem("s_ge")
        s_eo = sem("s_eo")
        s_flp = sem("s_flp")
        s_fls = sem("s_fls")
        s_flag = sem("s_flag")
        s_eoc = sem("s_eoc")
        s_eod = sems("s_eod")
        s_yg = sems("s_yg", 4)
        s_fin = sem("s_fin")
        s_out = sem("s_out")

        class Attention:

            def __init__(self, name, steps):
                self.general, self.steps = name == "g", steps
                self.score = sems(name + "_score")
                self.relu = sems(name + "_relu")
                self.mask = sems(name + "_mask")
                self.sum = sems(name + "_sum")
                self.step = sems(name + "_step")
                self.stT = sems(name + "_stT")
                self.stc = sems(name + "_stc")
                self.fin = sems(name + "_fin")
                self.res = sems(name + "_res")
                self.o = sems(name + "_o")
                self.oc = sems(name + "_oc")
                self.y = sems(name + "_y")
                self.x1 = sems(name + "_x1")
                self.st = sem(name + "_st")
                self.link = sem(name + "_link")
                self.SC = 2 * (steps + 1)
                self.MK = 2 * (steps - (not self.general))
                self.SM = steps + 1

            def masked(self, k):
                return self.general or k > 0

            def fine(self, k):
                return self.general or k >= COARSE

            def rows(self, k):
                return 2 * H if self.fine(k) else H

            def masks(self, k):
                return 2 * k if self.general else 2 * (k - 1)

            def loop(self, eng, body):
                if self.general:
                    with eng.Fori(0, self.steps) as k:
                        body(k)
                else:
                    for k in range(self.steps):
                        body(k)

        first = Attention("a", COARSE + FINE)
        general = Attention("g", GENERAL)

        def unless_converged(eng):
            eng.wait_ge(s_flag, 1)
            return eng.If(eng.value_load(flagi[0:1, 0:1], min_val=0, max_val=1) > 0)

        block = ctx.enter_context(nc.Block())

        halves = lambda w: w.rearrange("(k p) n -> p k n", p=P)
        one = lambda ap, n: ap.rearrange("(a n) -> a n", a=1)

        @block.sync
        def _(sp):
            for s in range(2):
                sp.sem_inc(s_eod[s], 16)
            x_v = x_d.rearrange("(c p) d -> p c d", p=P)
            sp.dma_start(cst[:], cst_d).then_inc(s_cst, 16)
            sp.dma_start(wk[:], halves(wk_d)).then_inc(s_wk, 16)
            sp.dma_start(wv[:], halves(wv_d)).then_inc(s_wv, 16)
            for k in range(4):
                sp.dma_start(x[:, 4 * k:4 * k + 4, :], x_v[:, 4 * k:4 * k + 4, :]).then_inc(s_x[k], 16)
            sp.dma_start(wq[:], halves(wq_d)).then_inc(s_w, 16)
            sp.dma_start(wo[:], halves(wo_d)).then_inc(s_w, 16)
            sp.wait_ge(s_zsrc, 1)
            half = CAP * E // 2
            for k in range(2):
                sp.dma_start(buf_d[k * half:(k + 1) * half, :].rearrange("(p r) d -> p (r d)", p=P),
                             x1[:, 0:half // P, :].rearrange("p c d -> p (c d)")).then_inc(s_zero, 16)

            def load_w1(e, s):
                sp.dma_start(w1[:, s], w1_d[bass.ds(e, 1)].rearrange("a (k p) f -> p (a k) f", p=P)).then_inc(s_w1[s], 16)

            def load_w2(e, s):
                sp.dma_start(w2[:, s], w2_d[bass.ds(e, 1)].rearrange("a (k p) d -> p (a k) d", p=P)).then_inc(s_w2[s], 16)
                sp.dma_start(b2b[:, s, :], b2_d[bass.ds(e, 1), :].to_broadcast([P, D])).then_inc(s_b2[s], 16)

            def load_rows(e, s):
                sp.dma_start(bufr[:, s], buf_d[bass.ds(e * CAP, CAP), :].rearrange("(c p) d -> p c d", p=P)).then_inc(s_buf[s], 16)

            for s in range(2):
                load_w1(s, s)
                load_w2(s, s)
            sp.wait_ge(s_disp, 16 * NCH)
            for s in range(2):
                load_rows(s, s)

            def store(e, s):
                sp.wait_ge(s_eoc, CT * (e + 2))
                sp.dma_start(eo_d[bass.ds(e * CAP, CAP), :].rearrange("(c p) d -> p c d", p=P), eo[:, s]).then_inc(s_eod[s], 16)

            with sp.Fori(0, E // 2 - 1) as i:
                for s in range(2):
                    e = 2 * i + s
                    sp.wait_ge(s_bt, e + 1)
                    load_rows(e + 2, s)
                    sp.wait_ge(s_wl, NQ * (e + 1))
                    load_w1(e + 2, s)
                    store(e, s)
                    load_w2(e + 2, s)
            for s in range(2):
                store(E - 2 + s, s)
            for k in range(4):
                sp.wait_ge(s_fin, 4 * (k + 1))
                sp.dma_start(out_d.rearrange("(c p) d -> p c d", p=P)[:, 4 * k:4 * k + 4, :],
                             x1[:, 4 * k:4 * k + 4, :]).then_inc(s_out, 16)
            sp.wait_ge(s_out, 64)

        @block.gpsimd
        def _(gp):
            nc.gpsimd.memset(KB[:], 0.0).then_inc(s_kb, 1)
            nc.gpsimd.memset(x1[:, 0:CAP * E // 2 // P, :], 0.0).then_inc(s_zsrc, 1)
            gp.wait_ge(s_bob, 1)
            with gp.Fori(0, CB) as i:
                for s in range(B):
                    c = i + CB * s
                    gp.wait_ge(s_xn[s], i + 1)
                    nc.gpsimd.tensor_tensor(x[:, bass.ds(c, 1), :], x[:, bass.ds(c, 1), :], bob[:].unsqueeze(1), ALU.add).then_inc(s_xb, 1)
            def weights_high(s, loads):
                for j, (full, high, _, q) in enumerate(QUARTERS):
                    if j % 4 == 0:
                        gp.wait_ge((s_w1 if j == 0 else s_w2)[s], loads)
                    nc.gpsimd.tensor_tensor(high[:, s, q], full[:, s, q], scale[:], ALU.mult).then_inc(s_wh, 1)

            nc.gpsimd.memset(scale[:], WS).then_inc(s_scale, 1)
            gp.wait_ge(s_scale, 1)
            gp.wait_ge(s_n2[0], 1)
            for s in range(2):
                weights_high(s, 16)
            gp.wait_ge(s_zero, 32)
            for s in range(B):
                gp.wait_ge(s_n2p[s], CB + 1)
            gp.wait_ge(s_idx, 1)
            for c in range(NCH):
                gp.indirect_dma_start(out=buf_d, out_offset=bass.IndirectOffsetOnAxis(ap=dsti[:, c:c + 1], axis=0),
                                      in_=x[:, c, :], in_offset=None).then_inc(s_disp, 16)
            with gp.Fori(1, E // 2) as i:
                for s in range(2):
                    gp.wait_ge(s_eo, CT * (2 * i + s - 1))
                    weights_high(s, 16 * (i + 1))
            for s in range(2):
                gp.wait_ge(s_eod[s], 16 * (E // 2 + 1))
            for c in range(NCH):
                gp.indirect_dma_start(out=yg[:, c, :], out_offset=None, in_=eo_d,
                                      in_offset=bass.IndirectOffsetOnAxis(ap=srci[:, c:c + 1], axis=0)).then_inc(s_yg[c // 4], 16)

        @block.scalar
        def _(act):
            for s in range(B):
                act.sem_inc(s_qc[s], 1)
                act.sem_inc(s_n2p[s], 1)
                for q in (first, general):
                    act.sem_inc(q.relu[s], q.SC)
            act.sem_inc(s_ge, FT)
            act.dma_start(cx[:], ctx_d.rearrange("b l d -> l b d")).then_inc(s_ctx, 16)
            for dst, src in ((rows[0:2, :], bq_d.rearrange("(g p) -> g p", p=P)),
                             (rows[2:4, :], bk_d.rearrange("(g p) -> g p", p=P)),
                             (rw[:], rw_d),
                             (b1r[:], b1_d.rearrange("e (f p) -> (e f) p", p=P)),
                             (bvr[:], one(bv_d, D)),
                             (gcol[:, 0:1], one(gx_d, 1).to_broadcast([P, 1])),
                             (gcol[:, 1:2], one(gf_d, 1).to_broadcast([P, 1])),
                             (bob[:], one(bo_d, D).to_broadcast([P, D]))):
                act.dma_start(dst, src).then_inc(s_small, 16)
            act.dma_start(sel[:], sel_d).then_inc(s_sel, 16)
            act.dma_start(neg32[:], neg_d).then_inc(s_neg, 16)
            act.wait_ge(s_cxT, 1)
            nc.scalar.copy(cxT[:].rearrange("p b k l -> p (b k l)"), X[1][:, 0:B * DH * L]).then_inc(s_cxc, 1)
            act.wait_ge(s_small, 16 * 8)
            nc.scalar.activation(tg[:], gcol[:], ACT.Tanh).then_inc(s_tg, 1)
            act.wait_ge(s_vp, 1)
            nc.scalar.copy(vs[:].rearrange("l b d -> l (b d)"), S[1][0:L, 0:B * D]).then_inc(s_vs, 1)
            act.wait_ge(s_var, 1)
            nc.scalar.activation(sd[:], mv[:, :, 1], ACT.Sqrt, bias=eps[:, 0:1]).then_inc(s_sd, 1)
            def turned_input(i, s):
                act.wait_ge(s_xt[s], i + 2)
                nc.scalar.copy(xnT[:, s].rearrange("p k t -> p (k t)"), X[s][:, 0:D]).then_inc(s_xc[s], 1)

            def queries(i, s):
                act.wait_ge(s_qp[s], i + 1)
                nc.scalar.activation(qT[:, 0, bass.ds(i * P + T * s, P)], S[s][:, 0:P], ACT.Identity,
                                     bias=bqs[:, 0:1], scale=HD ** -0.5)
                nc.scalar.activation(qT[:, 1, bass.ds(i * P + T * s, P)], S[s][:, P:2 * P], ACT.Identity,
                                     bias=bqs[:, 1:2], scale=HD ** -0.5).then_inc(s_qc[s], 1)

            for s in range(B):
                turned_input(0, s)
            with act.Fori(0, CB - 1) as i:
                for s in range(B):
                    queries(i, s)
                    turned_input(i + 1, s)
            for s in range(B):
                queries(CB - 1, s)

            def attend(q):
                def relu(i, s, k, out):
                    for n, (a, b) in enumerate(PIECES):
                        act.wait_ge(q.score[s], q.SC * i + 2 * k + n + 1)
                        nc.scalar.activation(out[:, s, a * P:b * P], S[s][:, a * P:b * P], ACT.Relu).then_inc(q.relu[s], 1)

                with act.Fori(0, CB) as i:
                    def step(k):
                        for s in range(B):
                            relu(i, s, k, r16)
                    q.loop(act, step)
                    for s in range(B):
                        relu(i, s, q.steps, r32)
                    for s in range(B):
                        act.wait_ge(q.o[s], i + 1)
                        nc.scalar.copy(oT[:, s].rearrange("p g t -> p (g t)"), S[s][:, 512:512 + D]).then_inc(q.oc[s], 1)

            attend(first)
            with unless_converged(act):
                attend(general)
            act.wait_ge(s_var, 2)
            nc.scalar.activation(sd[:], mv[:, :, 1], ACT.Sqrt, bias=eps[:, 0:1]).then_inc(s_sd, 1)
            with act.Fori(0, CB) as i:
                for s in range(B):
                    act.wait_ge(s_n2[s], i + 1)
                    nc.scalar.copy(x[:, bass.ds(i + CB * s, 1), :], xn[:, s:s + 1, :]).then_inc(s_n2p[s], 1)
                    act.wait_ge(s_n2t[s], i + 2)
                    nc.scalar.copy(xnT[:, s].rearrange("p k t -> p (k t)"), X[s][:, 0:D]).then_inc(s_n2c[s], 1)
            act.wait_ge(s_sh, 1)
            nc.scalar.activation(t3[:].rearrange("p c e -> p (c e)"), t3[:].rearrange("p c e -> p (c e)"), ACT.Exp).then_inc(s_ex, 1)
            nc.scalar.activation(warm_up[:], eps[:], ACT.Gelu)
            def gelu(e, s):
                act.wait_ge(s_b1e, e + 1)
                for f in range(FT):
                    bank = S[0][:, (f % 2) * 512:(f % 2) * 512 + CAP]
                    act.wait_ge(s_h, FT * e + f + 1)
                    nc.scalar.activation(hh[:, f, :], bank, ACT.Gelu, bias=b1e[:, s, f:f + 1], scale=1 / WS)
                    act.wait_ge(s_hl, FT * e + f + 1)
                    nc.scalar.activation(hT[:, f % 2, :], bank, ACT.Gelu, bias=b1e[:, s, f:f + 1], scale=1 / WS).then_inc(s_ge, 1)

            with act.Fori(0, E // 2) as i:
                for s in range(2):
                    gelu(2 * i + s, s)

        @block.vector
        def _(dve):
            for s in range(B):
                dve.sem_inc(s_lgc[s], 1)
                for q in (first, general):
                    dve.sem_inc(q.x1[s], 1)
                    dve.sem_inc(q.res[s], 1)
            dve.sem_inc(s_btc, DH)
            dve.sem_inc(s_hl, 2)
            dve.sem_inc(s_eoc, CT)
            link = Link(dve, s_setup)
            nc.vector.memset(eps[:], EPS)
            nc.vector.memset(off[:], 0.0)
            nc.vector.memset(nega[:], 0.0)
            nc.vector.memset(negb[:], 0.0)
            link(nc.vector.memset(partsT[:], 0.0))
            dve.wait_ge(s_cst, 16)
            nc.vector.tensor_copy(identb[:], ident)
            nc.vector.tensor_copy(trib[:], cst[:, C_TRI:C_TRI + P])
            nc.vector.tensor_copy(onesb[:], cst[:, C_ONE:C_ONE + P])
            nc.vector.tensor_copy(indb[:], ind32)
            link(nc.vector.tensor_copy(indh[:], ind32))
            def norm_scales():
                for c in range(NCH):
                    ins = nc.vector.bn_aggr(mv[:, c, :], stats[:, c, :])
                ins.then_inc(s_var, 1)

            for k in range(4):
                dve.wait_ge(s_x[k], 16)
                for c in range(4 * k, 4 * k + 4):
                    ins = nc.vector.bn_stats(stats[:, c, :], x[:, c, :])
            link(ins)
            norm_scales()
            dve.wait_ge(s_smT, 1)
            nc.vector.tensor_copy(bcol[:], X[0][:, 0:4])
            nc.vector.tensor_copy(rwT[:].rearrange("p k e -> p (k e)"), X[0][:, 8:8 + DH * E])
            link(nc.vector.tensor_copy(b1T[:], X[0][:, 64:64 + E * FT]))
            nc.vector.tensor_scalar(bqs[:], bcol[:, 0:DH], HD ** -0.5, None, ALU.mult).then_inc(s_smc, 1)
            dve.wait_ge(s_kp, 1)
            for n in range(B * DH):
                b, g = divmod(n, DH)
                ins = nc.vector.tensor_scalar(kT[:, b, g, :], S[0][:, n * P:n * P + L], bcol[:, DH + g:DH + g + 1], None,
                                              ALU.add, ALU.add, accum_out=ksum[:, n:n + 1])
            link(ins)
            link(nc.vector.tensor_scalar(ksum[:], ksum[:], 1.0 / L, None, ALU.mult))
            for n in range(B * DH):
                b, g = divmod(n, DH)
                ins = nc.vector.tensor_scalar(kT[:, b, g, :], kT[:, b, g, :], ksum[:, n:n + 1], None, ALU.subtract)
            ins.then_inc(s_kc, 1)
            dve.wait_ge(s_kc, 1)
            dve.wait_ge(s_kb, 1)
            for n in range(B * DH):
                b, g = divmod(n, DH)
                nc.vector.tensor_tensor(KB[:, b, g * KW:g * KW + HH * L].rearrange("p (h l) -> p h l", h=HH),
                                        kT[:, b, g, :].unsqueeze(1).to_broadcast([P, HH, L]),
                                        cst[:, C_HEAD:C_HEAD + HH].unsqueeze(2).to_broadcast([P, HH, L]), ALU.mult)
            for g in range(DH):
                dve.wait_ge(s_sp, g + 1)
                for b in range(B):
                    ins = nc.vector.tensor_tensor(
                        VB[:, b, g * KT:(g + 1) * KT, :].rearrange("p t (h d) -> p t h d", d=HD),
                        S[g][:, 0:KT * D].rearrange("p (t b h d) -> p t b h d", b=B, d=HD, h=HH)[:, :, b],
                        ind32[:, g * KT:(g + 1) * KT, g * HH:(g + 1) * HH].unsqueeze(3).to_broadcast([P, KT, HH, HD]), ALU.mult)
            ins.then_inc(s_vc, 1)
            dve.wait_ge(s_tg, 1)
            nc.vector.tensor_scalar(bob[:], bob[:], tg[:, 0:1], None, ALU.mult).then_inc(s_bob, 1)
            dve.wait_ge(s_neg, 16)
            nc.vector.tensor_copy(negb[0:2 * H, :], neg32[:])
            link(nc.vector.tensor_copy(nega[0:H, :], neg32[0:H, :]))
            dve.wait_ge(s_sd, 1)
            link(nc.vector.reciprocal(rs[:], sd[:]))
            with dve.Fori(0, CB) as i:
                for s in range(B):
                    c = i + CB * s
                    dve.wait_ge(s_xt[s], i + 1)
                    nc.vector.tensor_scalar(xn[:, s:s + 1, :], x[:, bass.ds(c, 1), :], mv[:, bass.ds(c, 1), 0:1].squeeze(2),
                                            rs[:, bass.ds(c, 1)], ALU.subtract, ALU.mult).then_inc(s_xn[s], 1)

            def attend(q):
                link = Link(dve, q.link)
                fine_links, coarse_links, guess_links, end_links = 3, 2, 1, 2
                per_chunk = B * (end_links + (q.steps * fine_links if q.general else
                                              guess_links + (COARSE - 1) * coarse_links + FINE * fine_links))

                def mask(i, s, k, n):
                    if not q.masked(k):
                        return
                    cols = slice(PIECES[n][0] * P, PIECES[n][1] * P)
                    dve.wait_ge(q.relu[s], q.SC * (i + 1) + 2 * k + n + 1)
                    ins = nc.vector.tensor_scalar(msk[:, s, cols], r16[:, s, cols], 0.0, None, ALU.is_gt)
                    if q.fine(k):
                        ins = nc.vector.scalar_tensor_tensor(rlo[:, s, cols], S[s][:, cols], 0.0, r16[:, s, cols],
                                                             ALU.max, ALU.subtract)
                    ins.then_inc(q.mask[s], 1)

                def newton(i, s, k, before):
                    link.at(per_chunk * i + before)
                    dve.wait_ge(q.sum[s], q.SM * i + k + 1)
                    total, count = X[s][:, 0:H], X[s][:, H:2 * H]
                    if not q.masked(k):
                        link(nc.vector.tensor_scalar(step[:, s, :], total, GUESS[0], GUESS[1], ALU.mult, ALU.add))
                        nc.vector.tensor_scalar(parts[:, s, 0:H], step[:, s, :], GUESS[2], None, ALU.min).then_inc(q.step[s], 1)
                    else:
                        link(nc.vector.tensor_scalar(cnt[:, s, :], count, 1.0, None, ALU.max))
                        link(nc.vector.reciprocal(cnt[:, s, :], cnt[:, s, :]))
                        if not q.fine(k):
                            nc.vector.scalar_tensor_tensor(parts[:, s, 0:H], total, -1.0, cnt[:, s, :],
                                                           ALU.add, ALU.mult).then_inc(q.step[s], 1)
                        else:
                            nc.vector.scalar_tensor_tensor(parts[:, s, 0:H], total, -1.0, cnt[:, s, :], ALU.add, ALU.mult)
                            link(nc.vector.scalar_tensor_tensor(step[:, s, :], total, -1.0, cnt[:, s, :], ALU.add, ALU.mult))
                            nc.vector.tensor_tensor(parts[:, s, H:2 * H], step[:, s, :], parts[:, s, 0:H],
                                                    ALU.subtract).then_inc(q.step[s], 1)
                    return link.n

                def turned(i, s, k):
                    dve.wait_ge(q.stT[s], q.steps * i + k + 1)
                    nc.vector.tensor_copy(partsT[0:q.rows(k), s, :], XT[s][0:q.rows(k), :]).then_inc(q.stc[s], 1)

                with dve.Fori(0, CB) as i:
                    if q.general:
                        with dve.Fori(0, q.steps) as k:
                            for s in range(B):
                                mask(i, s, k, 0)
                                mask(i, s, k, 1)
                                assert newton(i, s, k, B * fine_links * k + fine_links * s) == fine_links
                                turned(i, s, k)
                        before = B * fine_links * q.steps
                    else:
                        before = 0
                        for k in range(q.steps):
                            for s in range(B):
                                mask(i, s, k, 1)
                                before += newton(i, s, k, before)
                                if (s, k) != (B - 1, q.steps - 1):
                                    mask(i, 1 - s, k + s, 0)
                                turned(i, s, k)
                    link.at(per_chunk * i + before)
                    for s in range(B):
                        dve.wait_ge(q.relu[s], q.SC * (i + 2))
                        nc.vector.tensor_copy(r16[:, s, :], r32[:, s, :]).then_inc(q.fin[s], 1)
                    for s in range(B):
                        dve.wait_ge(q.fin[s], 2 * i + 1)
                        nc.vector.tensor_tensor(rlo[:, s, :], r32[:, s, :], r16[:, s, :], ALU.subtract).then_inc(q.fin[s], 1)
                    for s in range(B):
                        c = i + CB * s
                        dve.wait_ge(q.y[s], i + 1)
                        if not q.general:
                            dve.wait_ge(s_xb, B * i + s + 1)
                        nc.vector.scalar_tensor_tensor(x1[:, bass.ds(c, 1), :], S[s][:, 1024:1024 + D].unsqueeze(1), tg[:, 0:1],
                                                       x[:, bass.ds(c, 1), :], ALU.mult, ALU.add).then_inc(q.x1[s], 1)
                    for s in range(B):
                        dve.wait_ge(q.sum[s], q.SM * (i + 1))
                        nc.vector.tensor_scalar(step[:, s, :], X[s][:, 0:H], -1.0, None, ALU.add).then_inc(q.res[s], 1)
                    for s in range(B):
                        c = i + CB * s
                        dve.wait_ge(q.x1[s], i + 2)
                        nc.vector.bn_stats(stats[:, bass.ds(c, 1), :].squeeze(1), x1[:, bass.ds(c, 1), :].squeeze(1)).then_inc(q.st, 1)
                    for s in range(B):
                        dve.wait_ge(q.res[s], i + 2)
                        link(nc.vector.tensor_tensor(rest[:, s, :], step[:, s, :], step[:, s, :], ALU.mult))
                        link(nc.vector.tensor_tensor(off[:, s, :], off[:, s, :], rest[:, s, :], ALU.max))
                    assert q.general or link.n + before == per_chunk
                dve.wait_ge(q.st, NCH)

            dve.wait_ge(s_zero, 32)
            attend(first)
            link(nc.vector.tensor_reduce(out=flag[:, 0:1], in_=off[:].rearrange("p b h -> p (b h)"), axis=AX_X, op=ALU.max))
            nc.vector.tensor_scalar(flag[:, 1:2], flag[:, 0:1], LIMIT, None, ALU.is_gt).then_inc(s_flp, 1)
            dve.wait_ge(s_fls, 1)
            nc.vector.tensor_scalar(flagi[:], X[0][0:1, 0:1], 1.0, None, ALU.min).then_inc(s_flag, 1)
            with unless_converged(dve):
                attend(general)
            norm_scales()
            dve.wait_ge(s_sd, 2)
            link(nc.vector.reciprocal(rs[:], sd[:]))
            def norm(i, s):
                c = i + CB * s
                dve.wait_ge(s_n2t[s], i + 1)
                dve.wait_ge(s_n2p[s], i + 1)
                nc.vector.tensor_scalar(xn[:, s:s + 1, :], x1[:, bass.ds(c, 1), :], mv[:, bass.ds(c, 1), 0:1].squeeze(2),
                                        rs[:, bass.ds(c, 1)], ALU.subtract, ALU.mult).then_inc(s_n2[s], 1)

            def logits(i, s):
                dve.wait_ge(s_lgp[s], i + 1)
                nc.vector.tensor_copy(lg[:, bass.ds(i + CB * s, 1), :], S[s][:, 0:E].unsqueeze(1)).then_inc(s_lgc[s], 1)

            for s in range(B):
                norm(0, s)
            with dve.Fori(0, CB - 1) as i:
                for s in range(B):
                    norm(i + 1, s)
                    logits(i, s)
            for s in range(B):
                logits(CB - 1, s)
            for s in range(B):
                dve.wait_ge(s_lgc[s], CB + 1)
            wide = lambda ap: ap.unsqueeze(2).to_broadcast([P, NCH, E])
            each = lambda c: cst[:, c:c + E].unsqueeze(1).to_broadcast([P, NCH, E])
            link(nc.vector.tensor_reduce(out=lmax[:], in_=lg[:], axis=AX_X, op=ALU.max))
            nc.vector.tensor_tensor(t3[:], lg[:], wide(lmax[:]), ALU.subtract).then_inc(s_sh, 1)
            link(nc.vector.tensor_tensor(oh[:], lg[:], wide(lmax[:]), ALU.is_equal))
            link(nc.vector.tensor_tensor(oh[:], oh[:], each(C_REV), ALU.mult))
            link(nc.vector.tensor_reduce(out=t2[:], in_=oh[:], axis=AX_X, op=ALU.max))
            link(nc.vector.tensor_tensor(oh[:], wide(t2[:]), each(C_REV), ALU.is_equal))
            nc.vector.tensor_copy(ohb[:], oh[:]).then_inc(s_ohb, 1)
            dve.wait_ge(s_ex, 1)
            link(nc.vector.tensor_reduce(out=t2[:], in_=t3[:], axis=AX_X, op=ALU.add))
            link(nc.vector.reciprocal(gate[:], t2[:]))
            link(nc.vector.tensor_scalar(gate[:], gate[:], tg[:, 1:2], None, ALU.mult))
            link(nc.vector.tensor_tensor(t3[:], oh[:], each(C_BASE), ALU.mult))
            link(nc.vector.tensor_reduce(out=base[:], in_=t3[:], axis=AX_X, op=ALU.add))
            dve.wait_ge(s_pos, 1)
            link(nc.vector.tensor_tensor(t3[:], X[0][:, 0:NCH * E].rearrange("p (c e) -> p c e", e=E), oh[:], ALU.mult))
            link(nc.vector.tensor_reduce(out=pos[:], in_=t3[:], axis=AX_X, op=ALU.add))
            link(nc.vector.tensor_scalar(kept[:], pos[:], float(CAP), None, ALU.is_lt))
            link(nc.vector.tensor_tensor(gate[:], gate[:], kept[:], ALU.mult))
            link(nc.vector.tensor_tensor(dstf[:], base[:], pos[:], ALU.add))
            link(nc.vector.tensor_scalar(dstf[:], dstf[:], cst[:, C_ROW:C_ROW + 1], None, ALU.subtract))
            link(nc.vector.tensor_tensor(dstf[:], dstf[:], kept[:], ALU.mult))
            link(nc.vector.tensor_scalar(dsti[:], dstf[:], cst[:, C_ROW:C_ROW + 1], None, ALU.add))
            link(nc.vector.tensor_scalar(pos[:], pos[:], float(CAP - 1), None, ALU.min))
            nc.vector.tensor_tensor(srci[:], base[:], pos[:], ALU.add).then_inc(s_idx, 1)
            def weights_low(e, s, j):
                full, high, part, q = QUARTERS[j]
                dve.wait_ge(s_wh, NQ * e + j + 1)
                nc.vector.scalar_tensor_tensor(part[:, s, q], full[:, s, q], WS, high[:, s, q],
                                               ALU.mult, ALU.subtract).then_inc(s_wl, 1)

            def split_rows(e, s):
                dve.wait_ge(s_bt, e + 1)
                for k in range(DH):
                    nc.vector.tensor_copy(xh[:, s, k, :], X[k][:, 0:CAP]).then_inc(s_bth, 1)
                for k in range(DH):
                    dve.wait_ge(s_bth, DH * e + k + 1)
                    nc.vector.tensor_tensor(xl[:, s, k, :], X[k][:, 0:CAP], xh[:, s, k, :], ALU.subtract).then_inc(s_btc, 1)

            def expert(i, s, more):
                e = 2 * i + s
                for f in range(FT):
                    dve.wait_ge(s_ge, FT * (e + 1) + f + 1)
                    nc.vector.tensor_tensor(hl[:, f, :], hT[:, f % 2, :], hh[:, f, :], ALU.subtract).then_inc(s_hl, 1)
                    if more and f == 2:
                        nc.vector.tensor_copy(b1e[:, 1 - s, :], b1T[:, bass.ds(FT * (e + 1), FT)]).then_inc(s_b1e, 1)
                    if more:
                        for j in LOW_AT[f]:
                            weights_low(e + 1, 1 - s, j)
                        if f == TURN:
                            split_rows(e + 1, 1 - s)
                dve.wait_ge(s_b2[s], 16 * i + 16)
                dve.wait_ge(s_eod[s], 16 * (i + 1))
                for t in range(CT):
                    dve.wait_ge(s_eo, CT * e + t + 1)
                    nc.vector.scalar_tensor_tensor(eo[:, s, t, :], S[1][:, 512 * t:512 * t + D], 1 / WS, b2b[:, s, :],
                                                   ALU.mult, ALU.add).then_inc(s_eoc, 1)

            nc.vector.tensor_copy(b1e[:, 0, :], b1T[:, 0:FT]).then_inc(s_b1e, 1)
            for j in range(NQ):
                weights_low(0, 0, j)
            split_rows(0, 0)
            with dve.Fori(0, E // 2 - 1) as i:
                for s in range(2):
                    expert(i, s, True)
            expert(E // 2 - 1, 0, True)
            expert(E // 2 - 1, 1, False)
            for k in range(4):
                dve.wait_ge(s_yg[k], 64)
                for c in range(4 * k, 4 * k + 4):
                    nc.vector.scalar_tensor_tensor(x1[:, c, :], yg[:, c, :], gate[:, c:c + 1], x1[:, c, :],
                                                   ALU.mult, ALU.add).then_inc(s_fin, 1)

        @block.tensor
        def _(pe):
            mm = nc.tensor.matmul

            def acc(out, lhsT, rhs, first):
                return mm(out, lhsT, rhs, start=first, stop=True, skip_group_check=True)

            for s in range(B):
                pe.sem_inc(s_xt[s], 1)
                pe.sem_inc(s_n2t[s], 1)
            pe.wait_ge(s_cst, 16)
            pe.wait_ge(s_ctx, 16)
            for b in range(B):
                for k in range(DH):
                    n = b * DH + k
                    last = nc.tensor.transpose(X[1][:, n * L:(n + 1) * L], cx[:, b, k * P:(k + 1) * P], ident[0:L, 0:L])
            last.then_inc(s_cxT, 1)
            for _ in range(12):
                mm(S[0][:, 0:C_IND], ident, cst[:, 0:C_IND], start=True, stop=True)
            pe.wait_ge(s_small, 16 * 8)
            nc.tensor.transpose(X[0][:, 0:4], rows[0:4, :], ident[0:4, 0:4])
            for k in range(DH):
                nc.tensor.transpose(X[0][:, 8 + k * E:8 + (k + 1) * E], rw[:, k * P:(k + 1) * P], ident[0:E, 0:E])
            nc.tensor.transpose(X[0][:, 64:64 + E * FT], b1r[:], ident[0:E * FT, 0:E * FT]).then_inc(s_smT, 1)
            pe.wait_ge(s_cxc, 1)
            pe.wait_ge(s_wk, 16)
            for n in range(B * DH):
                b, g = divmod(n, DH)
                for k in range(DH):
                    last = mm(S[0][:, n * P:n * P + L], wk[:, k, g * P:(g + 1) * P], cxT[:, b, k, :], start=k == 0, stop=k == DH - 1)
            last.then_inc(s_kp, 1)
            pe.wait_ge(s_wv, 16)
            for b in range(B):
                out = S[1][0:L, b * D:(b + 1) * D]
                for k in range(DH):
                    mm(out, cxT[:, b, k, :], wv[:, k, :], start=k == 0, stop=False)
                last = mm(out, ones_row[:, 0:L], bvr[:], start=False, stop=True)
            last.then_inc(s_vp, 1)
            pe.wait_ge(s_kc, 1)
            pe.wait_ge(s_vs, 1)
            pe.wait_ge(s_sel, 16)
            for g in range(DH):
                for t in range(KT):
                    last = mm(S[g][:, t * D:(t + 1) * D].rearrange("p (b c) -> p b c", b=B), sel[:, t * P:(t + 1) * P],
                              vs[:, :, g * P:(g + 1) * P], start=True, stop=True)
                last.then_inc(s_sp, 1)
            pe.wait_ge(s_w, 32)
            pe.wait_ge(s_smc, 1)
            pe.wait_ge(s_vc, 1)

            def turn_input(i, s):
                pe.wait_ge(s_xn[s], i + 1)
                for k in range(DH):
                    last = nc.tensor.transpose(X[s][:, k * P:(k + 1) * P], xn[:, s, k * P:(k + 1) * P], ident)
                last.then_inc(s_xt[s], 1)

            def queries(i, s):
                pe.wait_ge(s_xc[s], i + 1)
                pe.wait_ge(s_qc[s], i + 1)
                for g in range(DH):
                    for k in range(DH):
                        last = mm(S[s][:, g * P:(g + 1) * P], wq[:, k, g * P:(g + 1) * P], xnT[:, s, k, :],
                                  start=k == 0, stop=k == DH - 1)
                last.then_inc(s_qp[s], 1)

            for s in range(B):
                turn_input(0, s)
            with pe.Fori(0, CB - 1) as i:
                for s in range(B):
                    queries(i, s)
                    turn_input(i + 1, s)
            for s in range(B):
                queries(CB - 1, s)
            for s in range(B):
                pe.wait_ge(s_qc[s], CB + 1)

            def attend(q):
                def scores(i, s):
                    pe.wait_ge(q.relu[s], q.SC * (i + 1))
                    pe.wait_ge(q.x1[s], i + 1)
                    for a, b in PIECES:
                        for t in range(a, b):
                            last = acc(S[s][:, t * P:(t + 1) * P], KB[:, s, t * P:(t + 1) * P],
                                       qT[:, t // KT, bass.ds(i * P + T * s, P)], t % 4 == 0)
                        last.then_inc(q.score[s], 1)

                def add(out, s, part, ind, n, first=False):
                    for t in range(*PIECES[n]):
                        last = acc(out, part[:, s, t * P:(t + 1) * P], ind[:, t, :], first and t == 0)
                    return last

                def sums(i, s, k, pieces=(0, 1)):
                    if 0 in pieces and (q.general or k == 0):
                        pe.wait_ge(q.res[s], i + 1)
                    for n in pieces:
                        pe.wait_ge(q.relu[s], q.SC * (i + 1) + 2 * k + n + 1)
                        last = add(X[s][:, 0:H], s, r16, indb, n, n == 0)
                        if q.masked(k):
                            pe.wait_ge(q.mask[s], q.MK * i + q.masks(k) + n + 1)
                            last = add(X[s][:, H:2 * H], s, msk, indb, n)
                        if q.fine(k):
                            last = add(X[s][:, 0:H], s, rlo, indh, n)
                    if 1 in pieces:
                        last.then_inc(q.sum[s], 1)

                def result_sums(i, s):
                    pe.wait_ge(q.fin[s], 2 * i + 2)
                    for n in range(2):
                        add(X[s][:, 0:H], s, r16, indb, n, n == 0)
                        last = add(X[s][:, 0:H], s, rlo, indh, n)
                    last.then_inc(q.sum[s], 1)

                def turn(i, s, k):
                    pe.wait_ge(q.step[s], q.steps * i + k + 1)
                    nc.tensor.transpose(XT[s][0:q.rows(k), :], parts[:, s, 0:q.rows(k)], identb[:]).then_inc(q.stT[s], 1)

                def move(i, s, k):
                    neg = negb if q.fine(k) else nega
                    pe.wait_ge(q.stc[s], q.steps * i + k + 1)
                    for a, b in PIECES:
                        for t in range(a, b):
                            last = acc(S[s][:, t * P:(t + 1) * P], neg[:, t * P:(t + 1) * P], partsT[:, s, :], False)
                        last.then_inc(q.score[s], 1)

                def keep_warm(s, k, n):
                    if q.general or k == 0:
                        return
                    for _ in range(n):
                        mm(X[s][:, 128:512], identb[:], negb[:, 0:512 - 128], start=True, stop=True)

                with pe.Fori(0, CB) as i:
                    for s in range(B):
                        scores(i, s)

                    def step(k):
                        sums(i, 0, k)
                        keep_warm(1, k, WARM[0])
                        turn(i, 0, k)
                        if q.fine(k):
                            sums(i, 1, k, (0,))
                            move(i, 0, k)
                            sums(i, 1, k, (1,))
                        else:
                            sums(i, 1, k)
                            move(i, 0, k)
                        keep_warm(0, k, WARM[1])
                        turn(i, 1, k)
                        move(i, 1, k)
                    q.loop(pe, step)
                    for s in range(B):
                        pe.wait_ge(q.relu[s], q.SC * (i + 2))
                        for t in range(NT):
                            g = t // KT
                            last = acc(S[s][:, 512 + g * P:512 + (g + 1) * P], VB[:, s, t, :], r32[:, s, t * P:(t + 1) * P], t == 0)
                        last.then_inc(q.o[s], 1)
                    for s in range(B):
                        pe.wait_ge(q.oc[s], i + 1)
                        for g in range(DH):
                            last = mm(S[s][:, 1024:1024 + D], oT[:, s, g, :], wo[:, g, :], start=g == 0, stop=g == DH - 1)
                        last.then_inc(q.y[s], 1)
                    for s in range(B):
                        result_sums(i, s)
                for s in range(B):
                    pe.wait_ge(q.x1[s], CB + 1)
                    pe.wait_ge(q.res[s], CB + 1)

            attend(first)
            pe.wait_ge(s_flp, 1)
            mm(X[0][:, 0:1], cst[:, C_ONE:C_ONE + P], flag[:, 1:2], start=True, stop=True).then_inc(s_fls, 1)
            with unless_converged(pe):
                attend(general)
            def turn_normed(i, s):
                pe.wait_ge(s_n2[s], i + 1)
                for k in range(DH):
                    last = nc.tensor.transpose(X[s][:, k * P:(k + 1) * P], xn[:, s, k * P:(k + 1) * P], ident)
                last.then_inc(s_n2t[s], 1)

            def logits(i, s):
                pe.wait_ge(s_n2c[s], i + 1)
                pe.wait_ge(s_lgc[s], i + 1)
                for k in range(DH):
                    last = mm(S[s][:, 0:E], xnT[:, s, k, :], rwT[:, k, :], start=k == 0, stop=k == DH - 1)
                last.then_inc(s_lgp[s], 1)

            for s in range(B):
                turn_normed(0, s)
            with pe.Fori(0, CB - 1) as i:
                for s in range(B):
                    logits(i, s)
                    turn_normed(i + 1, s)
            for s in range(B):
                logits(CB - 1, s)
            pe.wait_ge(s_ohb, 1)
            for s in range(B):
                pe.wait_ge(s_lgc[s], CB + 1)
            acc(X[0][:, 0:NCH * E], trib[:], ohb[:].rearrange("p c e -> p (c e)"), True)
            for c in range(1, NCH):
                last = acc(X[0][:, c * E:NCH * E].rearrange("p (c e) -> p c e", e=E), onesb[:],
                           ohb[:, c - 1:c, :].to_broadcast([P, NCH - c, E]), False)
            last.then_inc(s_pos, 1)
            pe.wait_ge(s_idx, 1)

            def turn_rows(i, s):
                pe.wait_ge(s_buf[s], 16 * i + 16)
                pe.wait_ge(s_btc, DH * (2 * i + s + 1))
                for k in range(DH):
                    for t in range(CT):
                        last = nc.tensor.transpose(X[k][:, t * P:(t + 1) * P], bufr[:, s, t, k * P:(k + 1) * P], ident)
                last.then_inc(s_bt, 1)

            def up(i, s, f):
                e = 2 * i + s
                if f == 0:
                    pe.wait_ge(s_wl, NQ * e + NQ // 2)
                    pe.wait_ge(s_btc, DH * (e + 2))
                pe.wait_ge(s_ge, FT * (e + 1) + f - 1)
                products = [(w, r, k) for k in range(DH) for w, r in ((w1h, xh), (w1h, xl), (w1l, xh))]
                for n, (w, r, k) in enumerate(products):
                    last = mm(S[0][:, (f % 2) * 512:(f % 2) * 512 + CAP], w1_part(w, s, k, f), r[:, s, k, :],
                              start=n == 0, stop=n == len(products) - 1)
                last.then_inc(s_h, 1)

            def down(i, s, f):
                e = 2 * i + s
                if f == 0:
                    pe.wait_ge(s_wl, NQ * (e + 1))
                    pe.wait_ge(s_eoc, CT * (e + 1))
                pe.wait_ge(s_hl, FT * e + f + 3)
                for t in range(CT):
                    for n, (h, w) in enumerate(((hh, w2h), (hh, w2l), (hl, w2h))):
                        last = mm(S[1][:, 512 * t:512 * t + D], h[:, f, t * P:(t + 1) * P], w2_part(w, s, f),
                                  start=f == 0 and n == 0, stop=f == FT - 1 and n == 2)
                    if f == FT - 1:
                        last.then_inc(s_eo, 1)

            def expert(i, s, more):
                for f in range(1, FT):
                    up(i, s, f)
                    if more and f == TURN:
                        turn_rows(i + s, 1 - s)
                    down(i, s, f - 1)
                if more:
                    up(i + s, 1 - s, 0)
                down(i, s, FT - 1)

            turn_rows(0, 0)
            up(0, 0, 0)
            with pe.Fori(0, E // 2 - 1) as i:
                for s in range(2):
                    expert(i, s, True)
            expert(E // 2 - 1, 0, True)
            expert(E // 2 - 1, 1, False)


_INPUTS = {
    "x": "x", "ctx_1024": "ctx", "g_xattn": "gx", "g_ffn": "gf",
    "L0_xattn_Wq": "wq", "L0_xattn_bq": "bq", "L0_xattn_Wk": "wk", "L0_xattn_bk": "bk",
    "L0_xattn_Wv": "wv", "L0_xattn_bv": "bv", "L0_xattn_Wo": "wo", "L0_xattn_bo": "bo",
    "L0_ffn_router_w": "rw", "L0_ffn_w1": "w1", "L0_ffn_b1": "b1", "L0_ffn_w2": "w2", "L0_ffn_b2": "b2",
}


def kernel(**inputs):
    import concourse.bacc as bacc
    from concourse.bass_utils import run_bass_kernel_spmd

    nc = bacc.Bacc("TRN2", target_bir_lowering=False, num_devices=1)
    arrays, args = {}, []
    for name, short in _INPUTS.items():
        a = np.ascontiguousarray(inputs[name])
        if name == "x":
            a = a.reshape(N, D)
        arrays[f"{short}_dram"] = a
    for name, a in constants().items():
        arrays[f"{name}_dram"] = a
    for name, a in arrays.items():
        args.append(nc.dram_tensor(name, a.shape, mybir.dt.from_np(a.dtype), kind="ExternalInput").ap())
    args.append(nc.dram_tensor("out_dram", (N, D), F32, kind="ExternalOutput").ap())
    flamingo_layer(nc, *args)
    r = run_bass_kernel_spmd(nc, [arrays], core_ids=[0])
    return r.results[0]["out_dram"].reshape(B, T, D)
```
